# Optimizing a Trainium2 kernel written in Bass

```python
import numpy as np
import jax
import jax.numpy as jnp

def _softmax(x, axis=-1):
    return jax.nn.softmax(x, axis=axis)

def _gelu(x):
    return jax.nn.gelu(x, approximate=True)

def _silu(x):
    return jax.nn.silu(x)

def _sigmoid(x):
    return jax.nn.sigmoid(x)

def _layernorm(x, axis=-1, eps=1e-05):
    m = jnp.mean(x, axis=axis, keepdims=True)
    v = jnp.var(x, axis=axis, keepdims=True)
    return (x - m) / jnp.sqrt(v + eps)

def _scatter_add(tgt, idx, src, axis=0):
    return tgt.at[idx].add(src)

def _segment_sum(src, seg, n):
    return jax.ops.segment_sum(src, seg, n)
kernel_name = 'mk_macaron_d2_jaxref_r8_68121d'

def setup_inputs(seed: int=0):
    np.random.seed(seed)
    _w = jnp.asarray

    def _L0_attn_setup():
        import jax, jax.numpy as jnp
        import numpy as np
        B, N, D, H = (2, 256, 128, 16)
        DH = D // H
        EPS = 1e-05

        def _lrpe(t, theta, n):
            idx = jnp.arange(n, dtype=t.dtype).reshape(1, n, 1)
            th = theta * idx
            return jnp.concatenate([t * jnp.cos(th), t * jnp.sin(th)], axis=-1)
        key = jax.random.key(seed)
        ks = jax.random.split(key, 8)
        x = jax.random.normal(ks[0], (B, N, D), dtype=jnp.float32)
        context = jax.random.normal(ks[1], (B, N, D), dtype=jnp.float32)
        Wqkvu = jax.random.normal(ks[2], (4 * D, D), dtype=jnp.float32) * 0.02
        bqkvu = jax.random.normal(ks[3], (4 * D,), dtype=jnp.float32) * 0.02
        Wout = jax.random.normal(ks[4], (D, D), dtype=jnp.float32) * 0.02
        bout = jax.random.normal(ks[5], (D,), dtype=jnp.float32) * 0.02
        theta = (10000.0 ** (-2.0 / D * jnp.arange(D, dtype=jnp.float32))).reshape(H, 1, DH)
        ln_w = jnp.ones((D,), dtype=jnp.float32)
        ln_b = jnp.zeros((D,), dtype=jnp.float32)
        return {'x': x, 'context': context, 'Wqkvu': Wqkvu, 'bqkvu': bqkvu, 'Wout': Wout, 'bout': bout, 'theta': theta, 'ln_w': ln_w, 'ln_b': ln_b}
    _L0_attn_in = _L0_attn_setup()

    def _L0_ffn_setup():
        import jax, jax.numpy as jnp
        import numpy as np
        B, S, H = (2, 256, 128)
        E, K = (16, 2)
        I = 64
        IS = I * 2
        key = jax.random.key(seed)
        ks = jax.random.split(key, 9)
        w = 0.02
        return {'hidden_states': jax.random.normal(ks[0], (B, S, H), jnp.float32), 'gate_weight': jax.random.normal(ks[1], (E, H), jnp.float32) / np.float32(np.sqrt(H)), 'We_gate': jax.random.normal(ks[2], (E, H, I), jnp.float32) * w, 'We_up': jax.random.normal(ks[3], (E, H, I), jnp.float32) * w, 'We_down': jax.random.normal(ks[4], (E, I, H), jnp.float32) * w, 'Ws_gate': jax.random.normal(ks[5], (H, IS), jnp.float32) * w, 'Ws_up': jax.random.normal(ks[6], (H, IS), jnp.float32) * w, 'Ws_down': jax.random.normal(ks[7], (IS, H), jnp.float32) * w}
    _L0_ffn_in = _L0_ffn_setup()

    def _L1_attn_setup():
        import jax, jax.numpy as jnp
        import numpy as np
        HIDDEN_DIM = 128
        NUM_HEADS = 16
        LN_EPS = 1e-06

        def _layernorm(x, scale, bias):
            mu = jnp.mean(x, axis=-1, keepdims=True)
            var = jnp.mean(jnp.square(x - mu), axis=-1, keepdims=True)
            return (x - mu) * jax.lax.rsqrt(var + LN_EPS) * scale + bias
        key = jax.random.key(seed)
        ks = jax.random.split(key, 4)
        B, S, D = (2, 256, HIDDEN_DIM)
        x = jax.random.normal(ks[0], (B, S, D), dtype=jnp.float32)
        scale = 1.0 / np.sqrt(D)
        wq = jax.random.normal(ks[1], (D, HIDDEN_DIM), dtype=jnp.float32) * scale
        wk = jax.random.normal(ks[2], (D, HIDDEN_DIM), dtype=jnp.float32) * scale
        wv = jax.random.normal(ks[3], (D, HIDDEN_DIM), dtype=jnp.float32) * scale
        ln_scale = jnp.ones((D,), dtype=jnp.float32)
        ln_bias = jnp.zeros((D,), dtype=jnp.float32)
        return {'x': x, 'ln_scale': ln_scale, 'ln_bias': ln_bias, 'wq': wq, 'wk': wk, 'wv': wv}
    _L1_attn_in = _L1_attn_setup()

    def _L1_ffn_setup():
        import jax, jax.numpy as jnp
        import numpy as np
        B, S, D = (4, 256, 128)
        N_EXPERTS, EXPERT_SIZE = (16, 32)
        WIDTH = N_EXPERTS * EXPERT_SIZE
        key = jax.random.key(seed)
        k_x, k_w1, k_w2, k_g = jax.random.split(key, 4)
        x = jax.random.normal(k_x, (B, S, D), dtype=jnp.float32)
        w1 = jax.random.normal(k_w1, (D, WIDTH), dtype=jnp.float32) / np.sqrt(D).astype(np.float32)
        b1 = jnp.zeros((WIDTH,), dtype=jnp.float32)
        w2 = jax.random.normal(k_w2, (WIDTH, D), dtype=jnp.float32) / np.sqrt(WIDTH).astype(np.float32)
        b2 = jnp.zeros((D,), dtype=jnp.float32)
        return {'x': x, 'w1': w1, 'b1': b1, 'w2': w2, 'b2': b2}
    _L1_ffn_in = _L1_ffn_setup()
    _d = {'L0_attn_x': _L0_attn_in['x'], 'L0_attn_context': _L0_attn_in['context'], 'L0_attn_Wqkvu': _L0_attn_in['Wqkvu'], 'L0_attn_bqkvu': _L0_attn_in['bqkvu'], 'L0_attn_Wout': _L0_attn_in['Wout'], 'L0_attn_bout': _L0_attn_in['bout'], 'L0_attn_theta': _L0_attn_in['theta'], 'L0_attn_ln_w': _L0_attn_in['ln_w'], 'L0_attn_ln_b': _L0_attn_in['ln_b'], 'L0_ffn_gate_weight': _L0_ffn_in['gate_weight'], 'L0_ffn_We_gate': _L0_ffn_in['We_gate'], 'L0_ffn_We_up': _L0_ffn_in['We_up'], 'L0_ffn_We_down': _L0_ffn_in['We_down'], 'L0_ffn_Ws_gate': _L0_ffn_in['Ws_gate'], 'L0_ffn_Ws_up': _L0_ffn_in['Ws_up'], 'L0_ffn_Ws_down': _L0_ffn_in['Ws_down'], 'L1_attn_ln_scale': _L1_attn_in['ln_scale'], 'L1_attn_ln_bias': _L1_attn_in['ln_bias'], 'L1_attn_wq': _L1_attn_in['wq'], 'L1_attn_wk': _L1_attn_in['wk'], 'L1_attn_wv': _L1_attn_in['wv'], 'L1_ffn_w1': _L1_ffn_in['w1'], 'L1_ffn_b1': _L1_ffn_in['b1'], 'L1_ffn_w2': _L1_ffn_in['w2'], 'L1_ffn_b2': _L1_ffn_in['b2']}
    _x0 = _d['L0_attn_x']
    _d['L0_attn_x'] = jax.random.normal(jax.random.fold_in(jax.random.key(seed), 1), (16, 512, 128), dtype=_x0.dtype)
    del _x0
    return _d

def reference(L0_attn_x, L0_attn_context, L0_attn_Wqkvu, L0_attn_bqkvu, L0_attn_Wout, L0_attn_bout, L0_attn_theta, L0_attn_ln_w, L0_attn_ln_b, L0_ffn_gate_weight, L0_ffn_We_gate, L0_ffn_We_up, L0_ffn_We_down, L0_ffn_Ws_gate, L0_ffn_Ws_up, L0_ffn_Ws_down, L1_attn_ln_scale, L1_attn_ln_bias, L1_attn_wq, L1_attn_wk, L1_attn_wv, L1_ffn_w1, L1_ffn_b1, L1_ffn_w2, L1_ffn_b2):

    def _L0_attn_ref(x, context, Wqkvu, bqkvu, Wout, bout, theta, ln_w, ln_b):
        import jax, jax.numpy as jnp
        import numpy as np
        B, N, D, H = (2, 256, 128, 16)
        DH = D // H
        EPS = 1e-05

        def _lrpe(t, theta, n):
            idx = jnp.arange(n, dtype=t.dtype).reshape(1, n, 1)
            th = theta * idx
            return jnp.concatenate([t * jnp.cos(th), t * jnp.sin(th)], axis=-1)
        b, n, d = x.shape
        qkvu = x @ Wqkvu.T + bqkvu
        q, k, v, u = jnp.split(qkvu, 4, axis=-1)
        tohead = lambda t: t.reshape(b, n, H, DH).transpose(0, 2, 1, 3)
        q, k, v = (tohead(q), tohead(k), tohead(v))
        q = jax.nn.silu(q)
        k = jax.nn.silu(k)
        q = _lrpe(q, theta, n)
        k = _lrpe(k, theta, n)
        qk = jnp.einsum('bhmd,bhnd->bhmn', q, k)
        out = jnp.einsum('bhmn,bhne->bhme', qk, v)
        out = out.transpose(0, 2, 1, 3).reshape(b, n, d)
        mu = jnp.mean(out, axis=-1, keepdims=True)
        var = jnp.var(out, axis=-1, keepdims=True)
        out = (out - mu) * jax.lax.rsqrt(var + EPS) * ln_w + ln_b
        out = u * out
        return out @ Wout.T + bout

    def _L0_ffn_ref(hidden_states, gate_weight, We_gate, We_up, We_down, Ws_gate, Ws_up, Ws_down):
        import jax, jax.numpy as jnp
        import numpy as np
        B, S, H = (2, 256, 128)
        E, K = (16, 2)
        I = 64
        IS = I * 2
        b, s, h = hidden_states.shape
        x = hidden_states.reshape(-1, h)
        T = x.shape[0]
        logits = x @ gate_weight.T
        scores = jax.nn.sigmoid(logits)
        topk_w, topk_idx = jax.lax.top_k(scores, K)
        topk_w = topk_w / (topk_w.sum(-1, keepdims=True) + 1e-20)
        comb = jnp.zeros((T, E), x.dtype).at[jnp.arange(T)[:, None], topk_idx].set(topk_w)
        g = jax.nn.silu(jnp.einsum('th,ehi->eti', x, We_gate))
        u = jnp.einsum('th,ehi->eti', x, We_up)
        ye = jnp.einsum('eti,eih->eth', g * u, We_down)
        y = jnp.einsum('te,eth->th', comb, ye).reshape(b, s, h)
        shared = jax.nn.silu(hidden_states @ Ws_gate) * (hidden_states @ Ws_up) @ Ws_down
        return y + shared

    def _L1_attn_ref(x, ln_scale, ln_bias, wq, wk, wv):
        import jax, jax.numpy as jnp
        import numpy as np
        HIDDEN_DIM = 128
        NUM_HEADS = 16
        LN_EPS = 1e-06

        def _layernorm(x, scale, bias):
            mu = jnp.mean(x, axis=-1, keepdims=True)
            var = jnp.mean(jnp.square(x - mu), axis=-1, keepdims=True)
            return (x - mu) * jax.lax.rsqrt(var + LN_EPS) * scale + bias
        bs, sl, fdim = x.shape
        h, hd = (NUM_HEADS, HIDDEN_DIM // NUM_HEADS)
        xn = _layernorm(x, ln_scale, ln_bias)
        q = (xn @ wq).reshape(bs, sl, h, hd).transpose(0, 2, 1, 3)
        k = (xn @ wk).reshape(bs, sl, h, hd).transpose(0, 2, 1, 3)
        v = (xn @ wv).reshape(bs, sl, h, hd).transpose(0, 2, 1, 3)
        scores = jnp.einsum('bhid,bhjd->bhij', q, k)
        probs = jax.nn.softmax(scores / jnp.sqrt(jnp.float32(HIDDEN_DIM)), axis=-1)
        out = jnp.einsum('bhij,bhjd->bhid', probs, v)
        out = out.transpose(0, 2, 1, 3).reshape(bs, sl, -1) + xn
        return out

    def _L1_ffn_ref(x, w1, b1, w2, b2):
        import jax, jax.numpy as jnp
        import numpy as np
        B, S, D = (4, 256, 128)
        N_EXPERTS, EXPERT_SIZE = (16, 32)
        WIDTH = N_EXPERTS * EXPERT_SIZE
        h = jax.nn.relu(jnp.einsum('bsd,dw->bsw', x, w1) + b1)
        return jnp.einsum('bsw,wd->bsd', h, w2) + b2
    x = L0_attn_x
    x = x + 0.5 * _L0_ffn_ref(_layernorm(x, axis=-1), L0_ffn_gate_weight, L0_ffn_We_gate, L0_ffn_We_up, L0_ffn_We_down, L0_ffn_Ws_gate, L0_ffn_Ws_up, L0_ffn_Ws_down)
    x = x + _L0_attn_ref(_layernorm(x, axis=-1), L0_attn_context, L0_attn_Wqkvu, L0_attn_bqkvu, L0_attn_Wout, L0_attn_bout, L0_attn_theta, L0_attn_ln_w, L0_attn_ln_b)
    x = x + 0.5 * _L0_ffn_ref(_layernorm(x, axis=-1), L0_ffn_gate_weight, L0_ffn_We_gate, L0_ffn_We_up, L0_ffn_We_down, L0_ffn_Ws_gate, L0_ffn_Ws_up, L0_ffn_Ws_down)
    x = x + 0.5 * _L1_ffn_ref(_layernorm(x, axis=-1), L1_ffn_w1, L1_ffn_b1, L1_ffn_w2, L1_ffn_b2)
    x = x + _L1_attn_ref(_layernorm(x, axis=-1), L1_attn_ln_scale, L1_attn_ln_bias, L1_attn_wq, L1_attn_wk, L1_attn_wv)
    x = x + 0.5 * _L1_ffn_ref(_layernorm(x, axis=-1), L1_ffn_w1, L1_ffn_b1, L1_ffn_w2, L1_ffn_b2)
    return x

_drawn_inputs = setup_inputs


def setup_inputs(seed=0):
    import zlib

    import numpy as np

    out = dict(_drawn_inputs(seed))
    spreads = {'L0_attn_ln_w': (1.0, 0.6),
     'L0_attn_ln_b': (0.0, 0.8),
     'L1_attn_ln_scale': (1.0, 0.2),
     'L1_attn_ln_bias': (0.0, 0.1),
     'L1_ffn_b1': (0.0, 0.468),
     'L1_ffn_b2': (0.0, 0.287)}
    factors = {'L0_attn_bqkvu': 6.311,
     'L0_ffn_gate_weight': 8.0,
     'L0_ffn_We_gate': 8.0,
     'L0_ffn_We_up': 8.0,
     'L0_ffn_We_down': 8.0,
     'L0_ffn_Ws_gate': 8.0,
     'L0_ffn_Ws_up': 8.0,
     'L0_ffn_Ws_down': 8.0,
     'L1_attn_wq': 4.222,
     'L1_attn_wk': 3.975}
    for name, (base, spread) in spreads.items():
        noise = np.random.default_rng([zlib.crc32(name.encode()), seed]).standard_normal(out[name].shape)
        drawn = base * np.exp(spread * noise) if base else spread * noise
        out[name] = jnp.asarray(drawn.astype(out[name].dtype))
    for name, factor in factors.items():
        out[name] = (out[name] * factor).astype(out[name].dtype)
    return out
```

```python
from contextlib import ExitStack

import numpy as np

import concourse.bass as bass
from concourse import mybir

F32 = mybir.dt.float32
F32R = mybir.dt.float32r
ALU = mybir.AluOpType
ACT = mybir.ActivationFunctionType
AX = mybir.AxisListType

P = 128
NB = 16
N = 512
T = N // P
D = 128
H, DH = 16, 8
E = 16
I_E = 64
TE = E * I_E // P
NT = TE + 1
FT = 4
GRP = 4
HG = H // GRP
EPS = 1e-5
EPS_IN = 1e-6
SM_SCALE = float(D) ** -0.5
BIG_ROUND = 12582912.0
TWO_PI = (6.28125, 0.0019350051879882812, 3.020991e-07)
PI_32 = 3.1415925


class Signal:

    def __init__(self, sem, per, pre=0):
        self.sem, self.per, self.pre = sem, per, pre

    def at(self, i, n):
        return i * self.per + (self.pre + n)


class Chain:

    def __init__(self, eng, sem, per):
        self.eng, self.sem, self.per = eng, sem, per
        self.base, self.n = 0, 0

    def enter(self, turn):
        self.outside = self.base + self.n
        self.base, self.n = turn * self.per + self.outside, 0

    def leave(self, turns):
        assert self.n == self.per, f"chain: {self.n} steps in a turn, {self.per} declared"
        self.base, self.n = self.outside + turns * self.per, 0

    def step(self, ins):
        ins.then_inc(self.sem, 1)
        self.n += 1

    def settle(self):
        self.eng.wait_ge(self.sem, self.base + self.n)


MAX_ROW = 3 * DH
MOE, ATT, MLP = "moe", "att", "mlp"
SLOTS = [(MOE, 0), (MOE, 1), (ATT, 0), (ATT, 1), (MOE, 0), (MOE, 1), (MLP, 0), (MLP, 1)]
NS = len(SLOTS)
TILES = {MOE: NT, ATT: 0, MLP: FT}


def before(q, weight):
    return sum(weight[SLOTS[s % NS][0]] for s in range(q))


G_W = {MOE: NT, ATT: 0, MLP: FT}
U_W = {MOE: NT, ATT: 0, MLP: 0}
C_W = {MOE: TE, ATT: 0, MLP: 0}
D_W = {MOE: NT, ATT: 1, MLP: FT}
M_W = {MOE: 1, ATT: 0, MLP: 0}
A_W = {MOE: 0, ATT: 1, MLP: 0}
N_MOE, N_ATT = before(NS, M_W), before(NS, A_W)
DVE_STEPS = NS + 21 * N_MOE + 4 * N_ATT
POOL_STEPS = NS + 3 * N_ATT


def build_front(nc, weights, x_dram, mid_dram, ident_dram, turns):
    w = weights
    with ExitStack() as ctx:
        def sb(name, shape, dt=F32):
            return ctx.enter_context(nc.sbuf_tensor(name, shape, dt))

        def ps(name, shape):
            return ctx.enter_context(nc.psum_tensor(name, shape, F32))

        def sig(name, per, pre=0):
            return Signal(ctx.enter_context(nc.semaphore(name)), per, pre)

        xin = [sb(f"xin{p}", [P, T, D]) for p in range(2)]
        xw = [sb(f"xw{p}", [P, T, D]) for p in range(2)]
        xb = [sb(f"xb{p}", [P, T, D]) for p in range(2)]
        z = sb("z", [P, T, D])
        xh = [sb(f"xh{p}", [P, T, P], F32R) for p in range(2)]
        xl = [sb(f"xl{p}", [P, T, P], F32R) for p in range(2)]
        stats = sb("stats", [P, T, 6])
        mv = sb("mv", [P, T, 2])
        vpe = sb("vpe", [P, T])
        rstd = sb("rstd", [P, T])
        nudge = sb("nudge", [P, 1])
        stats2 = sb("stats2", [P, T, 6])
        mv2 = sb("mv2", [P, T, 2])
        vpe2 = sb("vpe2", [P, T])
        rstd2 = sb("rstd2", [P, T])
        lb = sb("lb", [P, T, E])
        lg = sb("lg", [P, T, E])
        en = sb("en", [P, T, E])
        sc = sb("sc", [P, T, E])
        hit = sb("hit", [P, T, E])
        first = sb("first", [P, T, E])
        second = sb("second", [P, T, E])
        rest = sb("rest", [P, T, E])
        m1 = sb("m1", [P, T, 1])
        r1 = sb("r1", [P, T, 1])
        den = sb("den", [P, T, 1])
        comb = sb("comb", [P, T, E])
        comb2 = sb("comb2", [P, T, 2 * E])
        combh = sb("combh", [P, T, E], F32R)
        cT = [sb(f"cT{p}", [2 * E, T, P], F32R) for p in range(2)]
        sbuf_s = [sb(f"s{p}", [P, T, P]) for p in range(2)]
        su = [sb(f"su{k}", [P, T, P]) for k in range(2)]
        h = [sb(f"h{k}", [P, T, P]) for k in range(3)]
        kvu = sb("kvu", [P, T, 3 * D])
        kc = sb("kc", [P, 2, T, D])
        qa = sb("qa", [P, T, P])
        qc = sb("qc", [P, 2, T, P])
        kvm = sb("kvm", [P, 2, D])
        uw = sb("uw", [P, T, D])
        ub = sb("ub", [P, T, D])
        on = sb("on", [P, T, D])
        og = sb("og", [P, T, D])
        oT = sb("oT", [P, T, P])

        G = [ps(f"G{k}", [P, T, P]) for k in range(2)]
        U = [ps(f"U{k}", [P, T, P]) for k in range(2)]
        C = ps("C", [P, T, P])
        Y = ps("Y", [P, T, P])
        Z = ps("Z", [P, T, P])
        L = ps("L", [P, T, P])
        KVU = [G[1], U[0], U[1], C]

        x_loaded = [sig(f"x_loaded{p}", 16) for p in range(2)]
        stored = [sig(f"stored{p}", 16, 16) for p in range(2)]
        z_ready = sig("z_ready", NS)
        zT_ready = sig("zT_ready", NS)
        xh_ready = sig("xh_ready", NS)
        xl_ready = sig("xl_ready", NS)
        mv_ready = sig("mv_ready", NS)
        rstd_ready = sig("rstd_ready", NS)
        logits_ready = sig("logits_ready", N_MOE)
        lb_ready = sig("lb_ready", N_MOE)
        lg_ready = sig("lg_ready", N_MOE)
        score_ready = sig("score_ready", N_MOE)
        comb_ready = sig("comb_ready", N_MOE)
        combT_ready = sig("combT_ready", N_MOE)
        cT_ready = sig("cT_ready", N_MOE)
        gate_ready = sig("gate_ready", before(NS, G_W))
        act_done = sig("act_done", before(NS, G_W))
        up_ready = sig("up_ready", before(NS, U_W))
        up_used = sig("up_used", before(NS, U_W))
        weight_ready = sig("weight_ready", before(NS, C_W))
        h_ready = sig("h_ready", before(NS, C_W))
        down_done = sig("down_done", before(NS, D_W))
        res_done = sig("res_done", NS, 1)
        xb_ready = sig("xb_ready", before(NS, {MOE: 0, ATT: 1, MLP: 1}))
        q_mm = sig("q_mm", N_ATT)
        kvu_mm = sig("kvu_mm", T * N_ATT)
        kvu_out = sig("kvu_out", T * N_ATT)
        qa_ready = sig("qa_ready", N_ATT)
        ka_ready = sig("ka_ready", N_ATT)
        qc_ready = sig("qc_ready", N_ATT)
        kc_ready = sig("kc_ready", N_ATT)
        u_ready = sig("u_ready", N_ATT)
        kv_mm = sig("kv_mm", N_ATT)
        kvm_ready = sig("kvm_ready", N_ATT)
        o_mm = sig("o_mm", N_ATT)
        mv2_ready = sig("mv2_ready", N_ATT)
        rstd2_ready = sig("rstd2_ready", N_ATT)
        og_ready = sig("og_ready", N_ATT)
        oT_mm = sig("oT_mm", N_ATT)
        oT_ready = sig("oT_ready", N_ATT)
        dve_own = ctx.enter_context(nc.semaphore("dve_own"))
        pool_own = ctx.enter_context(nc.semaphore("pool_own"))

        xd = x_dram.rearrange("b (p t) d -> b p t d", p=P)
        md = mid_dram.rearrange("b (p t) d -> b p t d", p=P)
        block = ctx.enter_context(nc.Block())

        @block.sync
        def _(sp):
            for p in range(2):
                sp.dma_start(xin[p][:], xd[p]).then_inc(x_loaded[p].sem, 16)
                sp.dma_start(xw[p][:, 0, :], ident_dram).then_inc(stored[p].sem, 16)

            def store(i):
                for p in range(2):
                    sp.wait_ge(res_done.sem, res_done.at(i, NS - 2 + p + 1))
                    sp.dma_start(md[i * 2 + p], xw[p][:]).then_inc(stored[p].sem, 16)

            with sp.Fori(0, turns - 1) as i:
                for p in range(2):
                    sp.wait_ge(res_done.sem, res_done.at(i, p + 1))
                    sp.dma_start(xin[p][:], xd[i * 2 + (2 + p)]).then_inc(x_loaded[p].sem, 16)
                store(i)
            for p in range(2):
                sp.wait_ge(res_done.sem, res_done.at(turns - 1, p + 1))
                sp.dma_start(xin[p][:], xd[2 * turns - 2 + p]).then_inc(x_loaded[p].sem, 16)
            store(turns - 1)
            for p in range(2):
                sp.wait_ge(x_loaded[p].sem, 16 * (turns + 1))
                sp.wait_ge(stored[p].sem, 16 * (turns + 1))

        @block.gpsimd
        def _(pool):
            own = Chain(pool, pool_own, POOL_STEPS)

            def rsqrt(out, tmp, mean_var, i, ready, n, done):
                pool.wait_ge(ready.sem, ready.at(i, n + 1))
                own.step(nc.gpsimd.tensor_tensor(tmp[:], mean_var[:, :, 1], w["eps"][:], ALU.add))
                own.settle()
                nc.gpsimd.tensor_tensor(out[:], tmp[:], w["minus_half"][:], ALU.pow).then_inc(done.sem, 1)

            def prep(q, i):
                rsqrt(rstd, vpe, mv, i, mv_ready, q, rstd_ready)

            prep(0, 0)
            with pool.Fori(0, turns) as i:
                own.enter(i)
                for q, (kind, p) in enumerate(SLOTS):
                    if kind == ATT:
                        a = before(q, A_W)
                        pool.wait_ge(res_done.sem, res_done.at(i, q - 1))
                        nc.gpsimd.tensor_tensor(xb[p][:], xw[p][:], w["bout"][:], ALU.add).then_inc(xb_ready.sem, 1)
                        prep(q + 1, i)
                        pool.wait_ge(qa_ready.sem, qa_ready.at(i, a + 1))
                        own.step(nc.gpsimd.tensor_tensor(qc[:, 0], qa[:], w["cos_c"][:], ALU.mult))
                        nc.gpsimd.tensor_tensor(qc[:, 1], qa[:], w["sin_c"][:], ALU.mult).then_inc(qc_ready.sem, 1)
                        pool.wait_ge(kvu_out.sem, kvu_out.at(i, T * (a + 1)))
                        own.step(nc.gpsimd.tensor_tensor(uw[:], kvu[:, :, 2 * D:], w["lnw"][:], ALU.mult))
                        nc.gpsimd.tensor_tensor(ub[:], kvu[:, :, 2 * D:], w["lnb"][:], ALU.mult).then_inc(u_ready.sem, 1)
                        rsqrt(rstd2, vpe2, mv2, i, mv2_ready, a, rstd2_ready)
                    elif kind == MLP:
                        pool.wait_ge(res_done.sem, res_done.at(i, q - 1))
                        nc.gpsimd.tensor_tensor(xb[p][:], xw[p][:], w["b2h"][:], ALU.add).then_inc(xb_ready.sem, 1)
                        prep(q + 1, i)
                    else:
                        prep(q + 1, i)
                own.leave(turns)

        @block.scalar
        def _(act):
            def split_high(q, i):
                act.wait_ge(zT_ready.sem, zT_ready.at(i, q + 1))
                nc.scalar.activation(xh[q % 2][:], Z[:], ACT.Copy).then_inc(xh_ready.sem, 1)

            def logits_half(q, i):
                if SLOTS[q % NS][0] == MOE:
                    u = before(q, M_W)
                    act.wait_ge(logits_ready.sem, logits_ready.at(i, u + 1))
                    nc.scalar.activation(lb[:], L[:, :, E:2 * E], ACT.Copy).then_inc(lb_ready.sem, 1)

            def scores(q, i):
                if SLOTS[q % NS][0] == MOE:
                    u = before(q, M_W)
                    act.wait_ge(lg_ready.sem, lg_ready.at(i, u + 1))
                    nc.scalar.activation(en[:], lg[:], ACT.Exp, scale=-1.0).then_inc(score_ready.sem, 1)

            split_high(0, 0)
            logits_half(0, 0)
            scores(0, 0)
            with act.Fori(0, turns) as i:
                for q, (kind, p) in enumerate(SLOTS):
                    g0 = before(q, G_W)
                    if kind == MOE:
                        u0, u = before(q, U_W), before(q, M_W)
                        for n in range(NT):
                            act.wait_ge(gate_ready.sem, gate_ready.at(i, g0 + n + 1))
                            if n >= 2:
                                act.wait_ge(up_used.sem, up_used.at(i, u0 + n - 1))
                            nc.scalar.activation(sbuf_s[n % 2][:], G[n % 2][:], ACT.Silu).then_inc(act_done.sem, 1)
                            if n == 0:
                                act.wait_ge(combT_ready.sem, combT_ready.at(i, u + 1))
                                nc.scalar.activation(cT[u % 2][:], L[0:2 * E], ACT.Copy).then_inc(cT_ready.sem, 1)
                            if n == 4:
                                split_high(q + 1, i)
                            if n == 6:
                                logits_half(q + 1, i)
                            if n == 7:
                                scores(q + 1, i)
                    elif kind == ATT:
                        a = before(q, A_W)
                        act.wait_ge(q_mm.sem, q_mm.at(i, a + 1))
                        nc.scalar.activation(qa[:], G[0][:], ACT.Silu, bias=w["bq"][:]).then_inc(qa_ready.sem, 1)
                        act.wait_ge(kvu_out.sem, kvu_out.at(i, T * (a + 1)))
                        nc.scalar.activation(kvu[:, :, 0:D], kvu[:, :, 0:D], ACT.Silu).then_inc(ka_ready.sem, 1)
                        split_high(q + 1, i)
                        logits_half(q + 1, i)
                        act.wait_ge(oT_mm.sem, oT_mm.at(i, a + 1))
                        nc.scalar.activation(oT[:], U[0][:], ACT.Copy).then_inc(oT_ready.sem, 1)
                        scores(q + 1, i)
                    else:
                        for n in range(FT):
                            act.wait_ge(gate_ready.sem, gate_ready.at(i, g0 + n + 1))
                            if n >= 3:
                                act.wait_ge(down_done.sem, down_done.at(i, before(q, D_W) + n - 2))
                            nc.scalar.activation(h[n % 3][:], G[n % 2][:], ACT.Relu,
                                                 bias=w["b1"][:, n:n + 1]).then_inc(act_done.sem, 1)
                            if n == 2:
                                split_high(q + 1, i)
                        logits_half(q + 1, i)
                        scores(q + 1, i)

        @block.vector
        def _(dve):
            own = Chain(dve, dve_own, DVE_STEPS)

            def step(ins):
                own.step(ins)

            def source(q):
                return xin[q % NS] if q % NS < 2 else xw[q % 2]

            def wait_source(q, i):
                if q % NS < 2:
                    p = q % NS
                    dve.wait_ge(x_loaded[p].sem, x_loaded[p].at(i, 16 * (1 + q // NS)))
                else:
                    dve.wait_ge(res_done.sem, res_done.at(i, q - 1))

            def mean_var(src, st, m):
                for t in range(T):
                    ins = nc.vector.bn_stats(st[:, t], src[:, t])
                step(ins)

            def aggregate(st, m, done):
                own.settle()
                nc.vector.memset(nudge[:], 0.0)
                for t in range(T):
                    ins = nc.vector.bn_aggr(m[:, t], st[:, t])
                ins.then_inc(done.sem, 1)

            def prep_stats(q, i):
                wait_source(q, i)
                mean_var(source(q), stats, mv)

            def prep_aggregate(q, i):
                aggregate(stats, mv, mv_ready)

            def prep_normalise(q, i):
                dve.wait_ge(rstd_ready.sem, rstd_ready.at(i, q + 1))
                for t in range(T):
                    ins = nc.vector.tensor_scalar(z[:, t], source(q)[:, t], mv[:, t, 0:1], rstd[:, t:t + 1],
                                                  ALU.subtract, ALU.mult)
                ins.then_inc(z_ready.sem, 1)

            def prep_split_low(q, i):
                dve.wait_ge(xh_ready.sem, xh_ready.at(i, q + 1))
                nc.vector.tensor_tensor(xl[q % 2][:], Z[:], xh[q % 2][:], ALU.subtract).then_inc(xl_ready.sem, 1)

            def prep_logits(q, i):
                if SLOTS[q % NS][0] == MOE:
                    u = before(q, M_W)
                    dve.wait_ge(lb_ready.sem, lb_ready.at(i, u + 1))
                    nc.vector.tensor_tensor(lg[:], L[:, :, 0:E], lb[:], ALU.add).then_inc(lg_ready.sem, 1)

            def wide(t):
                return t[:].broadcast_to([P, T, E])

            def pick(values, best, mask, pos):
                step(nc.vector.tensor_reduce(best[:], values[:], AX.X, ALU.max))
                own.settle()
                step(nc.vector.tensor_tensor(hit[:], values[:], wide(best), ALU.is_equal))
                own.settle()
                step(nc.vector.tensor_tensor(hit[:], hit[:], w["ramp"][:], ALU.mult))
                own.settle()
                step(nc.vector.tensor_reduce(pos[:], hit[:], AX.X, ALU.max))
                own.settle()
                step(nc.vector.tensor_tensor(mask[:], hit[:], wide(pos), ALU.is_equal))

            def prep_top1(q, i):
                if SLOTS[q % NS][0] == MOE:
                    u = before(q, M_W)
                    dve.wait_ge(score_ready.sem, score_ready.at(i, u + 1))
                    step(nc.vector.tensor_scalar(en[:], en[:], 1.0, None, ALU.add))
                    own.settle()
                    step(nc.vector.reciprocal(sc[:], en[:]))
                    own.settle()
                    pick(sc, m1, first, r1)

            def prep_top2(q, i):
                if SLOTS[q % NS][0] == MOE:
                    own.settle()
                    step(nc.vector.scalar_tensor_tensor(out=rest[:], in0=first[:], scalar=-2.0, in1=sc[:],
                                                        op0=ALU.mult, op1=ALU.add))
                    own.settle()
                    pick(rest, m1, second, r1)

            def prep_weights(q, i):
                if SLOTS[q % NS][0] == MOE:
                    own.settle()
                    step(nc.vector.tensor_tensor(first[:], first[:], second[:], ALU.add))
                    own.settle()
                    step(nc.vector.tensor_tensor(rest[:], first[:], sc[:], ALU.mult))
                    own.settle()
                    step(nc.vector.tensor_reduce(den[:], rest[:], AX.X, ALU.add))
                    own.settle()
                    step(nc.vector.tensor_scalar(den[:], den[:], 1e-20, None, ALU.add))
                    own.settle()
                    step(nc.vector.reciprocal(den[:], den[:]))
                    own.settle()
                    step(nc.vector.tensor_tensor(comb[:], rest[:], wide(den), ALU.mult))
                    own.settle()
                    step(nc.vector.tensor_copy(combh[:], comb[:]))
                    own.settle()
                    step(nc.vector.tensor_copy(comb2[:, :, 0:E], combh[:]))
                    nc.vector.tensor_tensor(comb2[:, :, E:2 * E], comb[:], combh[:],
                                            ALU.subtract).then_inc(comb_ready.sem, 1)

            def residual(q, kind, p, i):
                dve.wait_ge(down_done.sem, down_done.at(i, before(q + 1, D_W)))
                if q < 2:
                    dve.wait_ge(stored[p].sem, stored[p].at(i, 0))
                if kind != MOE:
                    n = before(q + 1, {MOE: 0, ATT: 1, MLP: 1})
                    dve.wait_ge(xb_ready.sem, xb_ready.at(i, n))
                if kind == ATT:
                    ins = nc.vector.tensor_tensor(xw[p][:], Y[:], xb[p][:], ALU.add)
                else:
                    src = xb[p] if kind == MLP else source(q)
                    ins = nc.vector.scalar_tensor_tensor(out=xw[p][:], in0=Y[:], scalar=0.5, in1=src[:],
                                                         op0=ALU.mult, op1=ALU.add)
                ins.then_inc(res_done.sem, 1)

            nc.vector.memset(nudge[:], 0.0).then_inc(res_done.sem, 1)
            for f in (prep_stats, prep_aggregate, prep_normalise, prep_split_low, prep_logits, prep_top1,
                      prep_top2, prep_weights):
                f(0, 0)
            with dve.Fori(0, turns) as i:
                own.enter(i)
                for q, (kind, p) in enumerate(SLOTS):
                    if kind == MOE:
                        g0, u0, c0, d0 = (before(q, x) for x in (G_W, U_W, C_W, D_W))
                        for n in range(NT):
                            dve.wait_ge(act_done.sem, act_done.at(i, g0 + n + 1))
                            dve.wait_ge(up_ready.sem, up_ready.at(i, u0 + n + 1))
                            out = h[0] if n == 0 else su[n % 2]
                            if n >= 3:
                                dve.wait_ge(h_ready.sem, h_ready.at(i, c0 + n - 2))
                            elif c0 + n > 2:
                                dve.wait_ge(h_ready.sem, h_ready.at(i, c0))
                            nc.vector.tensor_tensor(out[:], U[n % 2][:], sbuf_s[n % 2][:],
                                                    ALU.mult).then_inc(up_used.sem, 1)
                            if n > 0:
                                dve.wait_ge(up_used.sem, up_used.at(i, u0 + n + 1))
                                dve.wait_ge(weight_ready.sem, weight_ready.at(i, c0 + n))
                                if n >= 3:
                                    dve.wait_ge(down_done.sem, down_done.at(i, d0 + n - 2))
                                nc.vector.tensor_tensor(h[n % 3][:], C[:], su[n % 2][:], ALU.mult).then_inc(h_ready.sem, 1)
                            if n == 0:
                                prep_stats(q + 1, i)
                            if n == 1:
                                prep_aggregate(q + 1, i)
                            if n == 2:
                                prep_normalise(q + 1, i)
                            if n == 4:
                                prep_split_low(q + 1, i)
                            if n == 6:
                                prep_logits(q + 1, i)
                            if n == 7:
                                prep_top1(q + 1, i)
                            if n == 8:
                                prep_top2(q + 1, i)
                    elif kind == ATT:
                        a = before(q, A_W)
                        for t in range(T):
                            dve.wait_ge(kvu_mm.sem, kvu_mm.at(i, T * a + t + 1))
                            nc.vector.tensor_tensor(kvu[:, t], KVU[t][:].rearrange("p a b -> p (a b)")[:, 0:3 * D],
                                                    w["bkvu"][:], ALU.add).then_inc(kvu_out.sem, 1)
                        prep_stats(q + 1, i)
                        prep_aggregate(q + 1, i)
                        dve.wait_ge(ka_ready.sem, ka_ready.at(i, a + 1))
                        step(nc.vector.tensor_tensor(kc[:, 0], kvu[:, :, 0:D], w["cos_t"][:], ALU.mult))
                        nc.vector.tensor_tensor(kc[:, 1], kvu[:, :, 0:D], w["sin_t"][:],
                                                ALU.mult).then_inc(kc_ready.sem, 1)
                        prep_normalise(q + 1, i)
                        dve.wait_ge(kv_mm.sem, kv_mm.at(i, a + 1))
                        nc.vector.tensor_tensor(kvm[:], G[0][:, 0:2], w["heads"][:], ALU.mult).then_inc(kvm_ready.sem, 1)
                        prep_split_low(q + 1, i)
                        dve.wait_ge(o_mm.sem, o_mm.at(i, a + 1))
                        mean_var(G[1], stats2, mv2)
                        aggregate(stats2, mv2, mv2_ready)
                        prep_logits(q + 1, i)
                        dve.wait_ge(rstd2_ready.sem, rstd2_ready.at(i, a + 1))
                        for t in range(T):
                            ins = nc.vector.tensor_scalar(on[:, t], G[1][:, t], mv2[:, t, 0:1], rstd2[:, t:t + 1],
                                                          ALU.subtract, ALU.mult)
                        step(ins)
                        own.settle()
                        dve.wait_ge(u_ready.sem, u_ready.at(i, a + 1))
                        step(nc.vector.tensor_tensor(on[:], on[:], uw[:], ALU.mult))
                        own.settle()
                        nc.vector.tensor_tensor(og[:], on[:], ub[:], ALU.add).then_inc(og_ready.sem, 1)
                        prep_top1(q + 1, i)
                        prep_top2(q + 1, i)
                    else:
                        prep_stats(q + 1, i)
                        prep_aggregate(q + 1, i)
                        prep_normalise(q + 1, i)
                        prep_split_low(q + 1, i)
                        prep_logits(q + 1, i)
                    residual(q, kind, p, i)
                    if kind == MLP:
                        prep_top1(q + 1, i)
                        prep_top2(q + 1, i)
                    prep_weights(q + 1, i)
                own.leave(turns)

        @block.tensor
        def _(pe):
            def flat(t):
                return t[:].rearrange("p a b -> p (a b)")

            def transposes(q, i):
                pe.wait_ge(z_ready.sem, z_ready.at(i, q + 1))
                for t in range(T):
                    mm = pe.transpose(Z[:, t], z[:, t], w["ident"][:])
                mm.then_inc(zT_ready.sem, 1)

            def logits(q, i):
                if SLOTS[q % NS][0] == MOE:
                    pe.wait_ge(xl_ready.sem, xl_ready.at(i, q + 1))
                    for t in range(T):
                        pe.matmul(L[:, t, 0:2 * E], xh[q % 2][:, t], w["router"][:], start=True, stop=False,
                                  skip_group_check=True)
                        mm = pe.matmul(L[:, t, 0:2 * E], xl[q % 2][:, t], w["router"][:], start=False, stop=True,
                                       skip_group_check=True)
                    mm.then_inc(logits_ready.sem, 1)

            def product(bank, wh, wl, q):
                a, b = flat(xh[q % 2]), flat(xl[q % 2])
                pe.matmul(flat(bank), wh, a, start=True, stop=False)
                pe.matmul(flat(bank), wl, a, start=False, stop=False)
                return pe.matmul(flat(bank), wh, b, start=False, stop=True)

            def down(hid, wd, first, i, q):
                if first:
                    pe.wait_ge(res_done.sem, res_done.at(i, q))
                for t in range(T):
                    mm = pe.matmul(Y[:, t], hid[:, t], wd, start=(first and t == 0), stop=True,
                                   skip_group_check=True)
                mm.then_inc(down_done.sem, 1)

            transposes(0, 0)
            logits(0, 0)
            with pe.Fori(0, turns) as i:
                for q, (kind, p) in enumerate(SLOTS):
                    g0, u0, c0 = (before(q, x) for x in (G_W, U_W, C_W))
                    pe.wait_ge(xl_ready.sem, xl_ready.at(i, q + 1))
                    if kind == MOE:
                        u = before(q, M_W)

                        def dowN_MOE(n):
                            if n == 0:
                                pe.wait_ge(up_used.sem, up_used.at(i, u0 + 1))
                            else:
                                pe.wait_ge(h_ready.sem, h_ready.at(i, c0 + n))
                            down(h[n % 3], w["wd"][:, n], n == 0, i, q)

                        for n in range(NT):
                            if n >= 2:
                                pe.wait_ge(act_done.sem, act_done.at(i, g0 + n - 1))
                            product(G[n % 2], w["wgh"][:, n], w["wgl"][:, n], q).then_inc(gate_ready.sem, 1)
                            if n >= 2:
                                pe.wait_ge(up_used.sem, up_used.at(i, u0 + n - 1))
                            product(U[n % 2], w["wuh"][:, n], w["wul"][:, n], q).then_inc(up_ready.sem, 1)
                            if n == 0:
                                pe.wait_ge(comb_ready.sem, comb_ready.at(i, u + 1))
                                for t in range(T):
                                    mm = pe.transpose(L[0:2 * E, t], comb2[:, t], w["ident"][:])
                                mm.then_inc(combT_ready.sem, 1)
                            if n >= 1:
                                dowN_MOE(n - 1)
                                if n == 1:
                                    pe.wait_ge(cT_ready.sem, cT_ready.at(i, u + 1))
                                pe.matmul(flat(C), w["pairs"][:, n - 1], flat(cT[u % 2]), start=True,
                                          stop=True).then_inc(weight_ready.sem, 1)
                            if n == 4:
                                transposes(q + 1, i)
                            if n == 6:
                                logits(q + 1, i)
                        dowN_MOE(NT - 1)
                    elif kind == ATT:
                        a = before(q, A_W)
                        product(G[0], w["wqh"][:], w["wql"][:], q).then_inc(q_mm.sem, 1)
                        for t in range(T):
                            o = flat(KVU[t])[:, 0:3 * D]
                            pe.matmul(o, xh[q % 2][:, t], w["wkvuh"][:], start=True, stop=False)
                            pe.matmul(o, xh[q % 2][:, t], w["wkvul"][:], start=False, stop=False)
                            pe.matmul(o, xl[q % 2][:, t], w["wkvuh"][:], start=False, stop=True).then_inc(kvu_mm.sem, 1)
                        pe.wait_ge(qa_ready.sem, qa_ready.at(i, a + 1))
                        pe.wait_ge(kc_ready.sem, kc_ready.at(i, a + 1))
                        for c in range(2):
                            for t in range(T):
                                mm = pe.matmul(G[0][:, c], kc[:, c, t], kvu[:, t, D:2 * D], start=(t == 0),
                                               stop=(t == T - 1), skip_group_check=True)
                        mm.then_inc(kv_mm.sem, 1)
                        transposes(q + 1, i)
                        pe.wait_ge(qc_ready.sem, qc_ready.at(i, a + 1))
                        pe.wait_ge(kvm_ready.sem, kvm_ready.at(i, a + 1))
                        for t in range(T):
                            for c in range(2):
                                mm = pe.matmul(G[1][:, t], qc[:, c, t], kvm[:, c], start=(c == 0), stop=(c == 1),
                                               skip_group_check=True)
                        mm.then_inc(o_mm.sem, 1)
                        logits(q + 1, i)
                        pe.wait_ge(og_ready.sem, og_ready.at(i, a + 1))
                        for t in range(T):
                            mm = pe.transpose(U[0][:, t], og[:, t], w["ident"][:])
                        mm.then_inc(oT_mm.sem, 1)
                        pe.wait_ge(oT_ready.sem, oT_ready.at(i, a + 1))
                        down(oT, w["wout"][:], True, i, q)
                    else:
                        for n in range(FT):
                            if n >= 2:
                                pe.wait_ge(act_done.sem, act_done.at(i, g0 + n - 1))
                            product(G[n % 2], w["w1h"][:, n], w["w1l"][:, n], q).then_inc(gate_ready.sem, 1)
                            if n >= 1:
                                pe.wait_ge(act_done.sem, act_done.at(i, g0 + n))
                                down(h[(n - 1) % 3], w["w2"][:, n - 1], n == 1, i, q)
                            if n == 2:
                                transposes(q + 1, i)
                        pe.wait_ge(act_done.sem, act_done.at(i, g0 + FT))
                        down(h[(FT - 1) % 3], w["w2"][:, FT - 1], False, i, q)
                        logits(q + 1, i)


SCHEDULE = [
    [], [("ot", -1, 3), ("qk", 0, 5)], [], [("nm", 0, 1), ("qk", 0, 6)],
    [], [("ot", 0, 0), ("qk", 0, 7)], [], [("nm", 0, 2), ("ft", -1, 0)],
    [("xt", 1, 0), ("g", -1, 0)], [("ot", 0, 1), ("qk", 1, 0)], [("qk", 1, 1), ("v", 1, 0)],
    [("nm", 0, 3), ("g", -1, 1)], [("g", -1, 2), ("qk", 1, 2), ("g", -1, 3)], [("ot", 0, 2), ("qk", 1, 3)],
    [("y", -1, 0)], [("nm", 1, 0), ("qk", 1, 4)]]
SMALL = sum(SCHEDULE, [])
STEPS = GRP * T
AHEAD = 5
UNITS = STEPS * HG
ST_BANKS, MX_BANKS = 2, 3
BACK_DVE = 2 * (3 + GRP)
BACK_POOL = 2 * 7


def build_back(nc, weights, mid_dram, out_dram, batches):
    w = weights
    with ExitStack() as ctx:
        def sb(name, shape, dt=F32):
            return ctx.enter_context(nc.sbuf_tensor("b_" + name, shape, dt))

        def ps(name, shape=(P, T, P)):
            return ctx.enter_context(nc.psum_tensor("b_" + name, list(shape), F32))

        def sig(name, per):
            return Signal(ctx.enter_context(nc.semaphore("b_" + name)), per)

        x = [sb(f"x{p}", [P, T, D]) for p in range(2)]
        z = sb("z", [P, T, D])
        xn = sb("xn", [P, T, D])
        xx = [sb(f"xx{p}", [P, T, D]) for p in range(2)]
        xh = [sb(f"xh{p}", [P, T, P], F32R) for p in range(2)]
        xl = [sb(f"xl{p}", [P, T, P], F32R) for p in range(2)]
        part = [sb(f"part{k}", [P, T, P], F32R) for k in range(2)]
        qt = [sb(f"qt{g}", [P, T, P], F32R) for g in range(GRP)]
        kt_ = [sb(f"kt{g}", [P, T, P], F32R) for g in range(GRP)]
        kz = [sb(f"kz{g}", [P, HG, T, P], F32R) for g in range(GRP)]
        qm = [sb(f"qm{k}", [P, T, P], F32R) for k in range(2)]
        nm = [sb(f"nm{k}", [P, T, P]) for k in range(2)]
        va = [sb(f"va{p}", [P, T, H, 32]) for p in range(2)]
        pr = [sb(f"pr{k}", [P, HG, N]) for k in range(2)]
        oTs = [sb(f"oTs{k}", [P, T, P]) for k in range(2)]
        rden = sb("rden", [P, T, HG, 1])
        osum = sb("osum", [P, T, D])
        xf = sb("xf", [P, T, D])
        xfb = sb("xfb", [P, T, D])
        zf = sb("zf", [P, T, D])
        fh = sb("fh", [P, T, P], F32R)
        fl = sb("fl", [P, T, P], F32R)
        hid = [sb(f"hid{n}", [P, T, P]) for n in range(FT)]
        res = [sb(f"res{p}", [P, T, D]) for p in range(2)]
        nudge = sb("nudge", [P, 1])
        norm = {k: (sb(f"st{k}", [P, T, 6]), sb(f"mv{k}", [P, T, 2]), sb(f"ve{k}", [P, T]), sb(f"rs{k}", [P, T, 1]))
                for k in ("1", "2", "f")}

        ST = [ps(f"ST{k}") for k in range(ST_BANKS)]
        MX = [ps(f"MX{k}") for k in range(MX_BANKS)]
        PV = ps("PV")
        M = [ps(f"M{k}") for k in range(2)]

        loaded = [sig(f"loaded{p}", 16) for p in range(2)]
        stored = [sig(f"stored{p}", 16) for p in range(2)]
        mv_ready = {k: sig(f"mv_ready{k}", 1) for k in norm}
        rs_ready = {k: sig(f"rs_ready{k}", 1) for k in norm}
        z1_ready = sig("z1_ready", 1)
        zf_ready = sig("zf_ready", 1)
        xn_ready = sig("xn_ready", 1)
        xx_ready = sig("xx_ready", 1)
        xfb_ready = sig("xfb_ready", 1)
        xf_ready = sig("xf_ready", 1)
        xh_ready = sig("xh_ready", 1)
        fh_ready = sig("fh_ready", 1)
        part_ready = sig("part_ready", 2 * GRP)
        spread = [sig(f"spread{g}", 16 * HG) for g in range(GRP)]
        cleared = ctx.enter_context(nc.semaphore("b_cleared"))
        scores_mm = sig("scores_mm", UNITS)
        exp_done = sig("exp_done", UNITS)
        pv_mm = sig("pv_mm", STEPS)
        pv_out = sig("pv_out", GRP)
        first_mm = sig("first_mm", UNITS)
        max_done = sig("max_done", UNITS)
        per = {"qk": 2 * GRP, "ot": GRP, "nm": GRP, "ft": 1, "g": FT, "y": 1, "xt": 1, "v": 1}
        made = {k: sig(f"made_{k}", n) for k, n in per.items()}
        used = {k: sig(f"used_{k}", n) for k, n in per.items()}
        dve_own = ctx.enter_context(nc.semaphore("b_dve_own"))
        pool_own = ctx.enter_context(nc.semaphore("b_pool_own"))

        md = mid_dram.rearrange("b (p t) d -> b p t d", p=P)
        od = out_dram.rearrange("b (p t) d -> b p t d", p=P)

        class Batch:

            def __init__(self, turn, off):
                self.turn, self.off = turn, off
                self.parity = off % 2
                known = isinstance(turn, int)
                self.exists = not known or 0 <= 2 * turn + off < batches

            def __add__(self, k):
                return Batch(self.turn, self.off + k)

            @property
            def number(self):
                return self.turn * 2 + self.off

            def at(self, signal, n):
                return self.turn * (2 * signal.per) + (self.off * signal.per + n)

            def at_own(self, signal, n):
                return self.turn * signal.per + ((self.off - self.parity) // 2 * signal.per + n)

        def bank_of(name, n):
            return M[[(a, c) for a, _, c in SMALL].index((name, n)) % 2]

        def program(eng, batch_steps, chain=None):
            for off in (-1, 0, 1):
                batch_steps(Batch(0, off))
            last = batches // 2 - 1
            if last > 1:
                with eng.Fori(1, last) as i:
                    if chain:
                        chain.enter(i - 1)
                    batch_steps(Batch(i, 0))
                    batch_steps(Batch(i, 1))
                    if chain:
                        chain.leave(last - 1)
            for off in (0, 1, 2):
                batch_steps(Batch(last, off))

        block = ctx.enter_context(nc.Block())

        @block.sync
        def _(sp):
            def spread_keys(B, g):
                if not B.exists:
                    return
                if isinstance(B.turn, int) and B.number == 0:
                    sp.wait_ge(cleared, g + 1)
                sp.wait_ge(used["qk"].sem, B.at(used["qk"], 2 * g + 1))
                for j in range(HG):
                    rows = slice(32 * j, 32 * j + 32)
                    sp.dma_start(kz[g][rows, j].bitcast(F32), kt_[g][rows].bitcast(F32)).then_inc(spread[g].sem, 16)

            def batch_steps(B):
                nxt, prv = B + 1, B + -1
                if nxt.exists:
                    p = nxt.parity
                    if not isinstance(nxt.turn, int) or nxt.number >= 2:
                        sp.wait_ge(xx_ready.sem, B.at(xx_ready, 0))
                    sp.dma_start(x[p][:], md[nxt.number]).then_inc(loaded[p].sem, 16)
                spread_keys(B, 3)
                spread_keys(nxt, 0)
                spread_keys(nxt, 1)
                if prv.exists:
                    p = prv.parity
                    sp.wait_ge(used["y"].sem, prv.at(used["y"], 1))
                    sp.dma_start(od[prv.number], res[p][:]).then_inc(stored[p].sem, 16)
                spread_keys(nxt, 2)

            program(sp, batch_steps)
            for p in range(2):
                sp.wait_ge(stored[p].sem, 16 * (batches // 2))

        @block.gpsimd
        def _(pool):
            own = Chain(pool, pool_own, BACK_POOL)

            def rsqrt(k, B, eps):
                _, mv, ve, rs = norm[k]
                pool.wait_ge(mv_ready[k].sem, B.at(mv_ready[k], 1))
                own.step(nc.gpsimd.tensor_tensor(ve[:], mv[:, :, 1], w[eps][:], ALU.add))
                own.settle()
                nc.gpsimd.tensor_tensor(rs[:, :, 0], ve[:], w["minus_half"][:], ALU.pow).then_inc(rs_ready[k].sem, 1)

            def normalise(k, src, B):
                _, mv, _, rs = norm[k]
                pool.wait_ge(rs_ready[k].sem, B.at(rs_ready[k], 1))
                own.step(nc.gpsimd.tensor_tensor(z[:], src[:], mv[:, :, 0:1].broadcast_to([P, T, D]), ALU.subtract))
                own.settle()
                return nc.gpsimd.tensor_tensor(z[:], z[:], rs[:].broadcast_to([P, T, D]), ALU.mult)

            def batch_steps(B):
                nxt, prv = B + 1, B + -1
                if nxt.exists:
                    rsqrt("1", nxt, "eps")
                    normalise("1", x[nxt.parity], nxt).then_inc(z1_ready.sem, 1)
                if prv.exists:
                    pool.wait_ge(used["ot"].sem, prv.at(used["ot"], GRP))
                    if not isinstance(prv.turn, int) or prv.number >= 1:
                        pool.wait_ge(xfb_ready.sem, prv.at(xfb_ready, 0))
                        pool.wait_ge(zf_ready.sem, prv.at(zf_ready, 0))
                    nc.gpsimd.tensor_tensor(xf[:], osum[:], xx[prv.parity][:], ALU.add).then_inc(xf_ready.sem, 1)
                    rsqrt("f", prv, "eps")
                if nxt.exists:
                    rsqrt("2", nxt, "eps_in")
                    own.step(normalise("2", z, nxt))
                    own.settle()
                    own.step(nc.gpsimd.tensor_tensor(xn[:], z[:], w["lns"][:], ALU.mult))
                    own.settle()
                    nc.gpsimd.tensor_tensor(xn[:], xn[:], w["lnsb"][:], ALU.add).then_inc(xn_ready.sem, 1)
                    pool.wait_ge(xn_ready.sem, nxt.at(xn_ready, 1))
                    nc.gpsimd.tensor_tensor(xx[nxt.parity][:], x[nxt.parity][:], xn[:],
                                            ALU.add).then_inc(xx_ready.sem, 1)
                if prv.exists:
                    pool.wait_ge(xf_ready.sem, prv.at(xf_ready, 1))
                    nc.gpsimd.tensor_tensor(xfb[:], xf[:], w["b2h"][:], ALU.add).then_inc(xfb_ready.sem, 1)

            for g in range(GRP):
                nc.gpsimd.memset(kz[g][:].bitcast(F32), 0.0).then_inc(cleared, 1)
            for p in range(2):
                own.step(nc.gpsimd.memset(va[p][:], 0.0))
                own.settle()
                own.step(nc.gpsimd.memset(va[p][:, :, :, DH:DH + 1], 1.0))
            own.settle()
            program(pool, batch_steps, own)

        @block.scalar
        def _(act):
            def small(B, name, n):
                if not B.exists:
                    return
                p = B.parity
                act.wait_ge(made[name].sem, B.at(made[name], n + 1))
                m = bank_of(name, n)
                if name == "qk":
                    if not isinstance(B.turn, int) or B.number * 2 * GRP + n >= 2:
                        act.wait_ge(used["qk"].sem, B.at(used["qk"], n - 1))
                    if n % 2 == 1:
                        ins = nc.scalar.activation(part[0][:], m[:], ACT.Copy, scale=w["keep"][:, 0:1])
                    else:
                        ins = nc.scalar.activation(part[1][:], m[:], ACT.Identity, scale=w["keep"][:, 2:3],
                                                   bias=w["keep"][:, 4:5])
                    ins.then_inc(part_ready.sem, 1)
                elif name == "xt":
                    nc.scalar.activation(xh[p][:], m[:], ACT.Copy).then_inc(xh_ready.sem, 1)
                elif name == "ft":
                    nc.scalar.activation(fh[:], m[:], ACT.Copy).then_inc(fh_ready.sem, 1)
                elif name == "v":
                    nc.scalar.activation(va[p][:, :, :, 0:DH], m[:].rearrange("p t (h e) -> p t h e", h=H),
                                         ACT.Copy).then_inc(used["v"].sem, 1)
                elif name == "g":
                    nc.scalar.activation(hid[n][:], m[:], ACT.Relu, bias=w["b1"][:, n:n + 1]).then_inc(used["g"].sem, 1)

            def weights_out(B, g):
                if B.exists:
                    act.wait_ge(pv_mm.sem, B.at(pv_mm, T * (g + 1)))
                    nc.scalar.activation(oTs[g % 2][:], PV[:], ACT.Copy).then_inc(pv_out.sem, 1)

            def batch_steps(B):
                nxt, prv = B + 1, B + -1
                for k in range(STEPS):
                    for j in range(HG):
                        if B.exists:
                            u = k * HG + j
                            act.wait_ge(scores_mm.sem, B.at(scores_mm, u + 1))
                            if j == 0 and (k >= 2 or not isinstance(B.turn, int) or B.number > 0):
                                act.wait_ge(pv_mm.sem, B.at(pv_mm, k - 1))
                            nc.scalar.activation(pr[k % 2][:, j], ST[u % ST_BANKS][:].rearrange("p a b -> p (a b)"),
                                                 ACT.Exp, scale=SM_SCALE).then_inc(exp_done.sem, 1)
                        if j == 1 and k % T == 0:
                            if k == 0:
                                weights_out(prv, GRP - 1)
                            else:
                                weights_out(B, k // T - 1)
                        if j == 1:
                            for name, rel, n in SCHEDULE[k]:
                                if name not in ("ot", "nm", "y"):
                                    small(B + rel, name, n)

            program(act, batch_steps)

        @block.vector
        def _(dve):
            own = Chain(dve, dve_own, BACK_DVE)

            def stats(k, src):
                st, mv, _, _ = norm[k]
                for t in range(T):
                    ins = nc.vector.bn_stats(st[:, t], src[:, t])
                own.step(ins)
                own.settle()
                nc.vector.memset(nudge[:], 0.0)
                for t in range(T):
                    ins = nc.vector.bn_aggr(mv[:, t], st[:, t])
                ins.then_inc(mv_ready[k].sem, 1)

            def normalise(k, out, src, B, done):
                _, mv, _, rs = norm[k]
                dve.wait_ge(rs_ready[k].sem, B.at(rs_ready[k], 1))
                for t in range(T):
                    ins = nc.vector.tensor_scalar(out[:, t], src[:, t], mv[:, t, 0:1], rs[:, t],
                                                  ALU.subtract, ALU.mult)
                ins.then_inc(done.sem, 1)

            def small(B, name, n):
                if not B.exists:
                    return
                p = B.parity
                m = bank_of(name, n)
                if name == "qk":
                    dve.wait_ge(part_ready.sem, B.at(part_ready, n + 1))
                    out, c = (kt_ if n % 2 == 0 else qt)[n // 2], 3 if n % 2 == 0 else 1
                    if n % 2 == 0 and (not isinstance(B.turn, int) or B.number > 0):
                        dve.wait_ge(spread[n // 2].sem, B.at(spread[n // 2], 0))
                    nc.vector.scalar_tensor_tensor(out=out[:], in0=m[:], scalar=w["keep"][:, c:c + 1],
                                                   in1=part[1 - n % 2][:], op0=ALU.mult,
                                                   op1=ALU.add).then_inc(used["qk"].sem, 1)
                elif name == "xt":
                    dve.wait_ge(xh_ready.sem, B.at(xh_ready, 1))
                    nc.vector.tensor_tensor(xl[p][:], m[:], xh[p][:], ALU.subtract).then_inc(used["xt"].sem, 1)
                elif name == "ft":
                    dve.wait_ge(fh_ready.sem, B.at(fh_ready, 1))
                    nc.vector.tensor_tensor(fl[:], m[:], fh[:], ALU.subtract).then_inc(used["ft"].sem, 1)
                elif name == "nm":
                    dve.wait_ge(made["nm"].sem, B.at(made["nm"], n + 1))
                    nc.vector.tensor_tensor(qm[n % 2][:], qt[n][:], m[:], ALU.subtract).then_inc(used["nm"].sem, 1)
                elif name == "ot":
                    dve.wait_ge(made["ot"].sem, B.at(made["ot"], n + 1))
                    if n > 0 or not isinstance(B.turn, int) or B.number > 0:
                        dve.wait_ge(used["ot"].sem, B.at(used["ot"], n))
                    o = m[:].rearrange("p t (j r) -> p t j r", j=HG)
                    if n == 0 and (not isinstance(B.turn, int) or B.number > 0):
                        dve.wait_ge(xf_ready.sem, B.at(xf_ready, 0))
                    own.step(nc.vector.reciprocal(rden[:], o[:, :, :, DH:DH + 1]))
                    own.settle()
                    for t in range(T):
                        ins = nc.vector.tensor_tensor(
                            osum[:, t, n * HG * DH:(n + 1) * HG * DH].rearrange("p (j e) -> p j e", j=HG),
                            o[:, t, :, 0:DH], rden[:, t].broadcast_to([P, HG, DH]), ALU.mult)
                    ins.then_inc(used["ot"].sem, 1)
                elif name == "y":
                    dve.wait_ge(made["y"].sem, B.at(made["y"], 1))
                    dve.wait_ge(xfb_ready.sem, B.at(xfb_ready, 1))
                    if not isinstance(B.turn, int) or B.number >= 2:
                        dve.wait_ge(stored[p].sem, B.at_own(stored[p], 0))
                    nc.vector.scalar_tensor_tensor(out=res[p][:], in0=m[:], scalar=0.5, in1=xfb[:], op0=ALU.mult,
                                                   op1=ALU.add).then_inc(used["y"].sem, 1)

            def side(B, k):
                nxt, prv = B + 1, B + -1
                if k == 0 and nxt.exists:
                    p = nxt.parity
                    dve.wait_ge(loaded[p].sem, nxt.at_own(loaded[p], 16))
                    stats("1", x[p])
                if k == 2 and prv.exists:
                    dve.wait_ge(xf_ready.sem, prv.at(xf_ready, 1))
                    stats("f", xf)
                if k == 4 and nxt.exists:
                    dve.wait_ge(z1_ready.sem, nxt.at(z1_ready, 1))
                    stats("2", z)
                if k == 6 and prv.exists:
                    normalise("f", zf, xf, prv, zf_ready)

            def maximum(B, u):
                g, j, t = u // (HG * T), u // T % HG, u % T
                dve.wait_ge(first_mm.sem, B.at(first_mm, u + 1))
                c = 32 * j + MAX_ROW
                nc.vector.tensor_reduce(nm[g % 2][:, t, c:c + 1], MX[u % MX_BANKS][:].rearrange("p a b -> p (a b)"), AX.X,
                                        ALU.max).then_inc(max_done.sem, 1)

            def batch_steps(B):
                for k in range(STEPS):
                    C, s = (B, k + AHEAD) if k + AHEAD < STEPS else (B + 1, k + AHEAD - STEPS)
                    if C.exists:
                        for t in range(2):
                            maximum(C, s * T + t)
                    for name, rel, n in SCHEDULE[k]:
                        if name == "nm":
                            small(B + rel, name, n)
                    if C.exists:
                        for t in range(2, T):
                            maximum(C, s * T + t)
                    for name, rel, n in SCHEDULE[k]:
                        if name not in ("v", "g", "nm"):
                            small(B + rel, name, n)
                    side(B, k)

            for k in range(2):
                own.step(nc.vector.memset(nm[k][:], 0.0))
            own.settle()
            program(dve, batch_steps, own)

        @block.tensor
        def _(pe):
            def flat(t):
                return t[:].rearrange("p a b -> p (a b)")

            def product(bank, wh, wl, a, b):
                pe.matmul(flat(bank), wh, flat(a), start=True, stop=False)
                pe.matmul(flat(bank), wl, flat(a), start=False, stop=False)
                return pe.matmul(flat(bank), wh, flat(b), start=False, stop=True)

            def wait_small_bank(B, pos):
                here = B + -SMALL[pos][1]
                for back in range(2, len(SMALL), 2):
                    before_name, before_rel, before_n = SMALL[pos - back]
                    other = here + (before_rel - (1 if pos < back else 0))
                    if other.exists:
                        pe.wait_ge(used[before_name].sem, other.at(used[before_name], before_n + 1))
                        break

            def mlp_out(B, t):
                if not B.exists:
                    return
                m = bank_of("y", 0)
                if t == 0:
                    wait_small_bank(B, SMALL.index(("y", -1, 0)))
                    pe.wait_ge(used["g"].sem, B.at(used["g"], FT))
                for f in range(FT):
                    mm = pe.matmul(m[:, t], hid[f][:, t], w["w2"][:, f], start=(f == 0), stop=(f == FT - 1),
                                   skip_group_check=True)
                if t == T - 1:
                    mm.then_inc(made["y"].sem, 1)

            def small(B, name, n):
                if not B.exists:
                    return
                p = B.parity
                pos = [(a, c) for a, _, c in SMALL].index((name, n))
                m = M[pos % 2]
                wait_small_bank(B, pos)
                if name == "qk":
                    g = n // 2
                    pe.wait_ge(used["xt"].sem, B.at(used["xt"], 1))
                    r = "kr" if n % 2 == 0 else "qr"
                    mm = product(m, w[r + "h"][:, g], w[r + "l"][:, g], xh[p], xl[p])
                elif name == "xt":
                    pe.wait_ge(xn_ready.sem, B.at(xn_ready, 1))
                    for t in range(T):
                        mm = pe.transpose(m[:, t], xn[:, t], w["ident"][:])
                elif name == "ft":
                    pe.wait_ge(zf_ready.sem, B.at(zf_ready, 1))
                    for t in range(T):
                        mm = pe.transpose(m[:, t], zf[:, t], w["ident"][:])
                elif name == "v":
                    pe.wait_ge(used["xt"].sem, B.at(used["xt"], 1))
                    for t in range(T):
                        pe.matmul(m[:, t], xh[p][:, t], w["wvh"][:], start=True, stop=False, skip_group_check=True)
                        pe.matmul(m[:, t], xh[p][:, t], w["wvl"][:], start=False, stop=False, skip_group_check=True)
                        mm = pe.matmul(m[:, t], xl[p][:, t], w["wvh"][:], start=False, stop=True,
                                       skip_group_check=True)
                elif name == "nm":
                    pe.wait_ge(max_done.sem, B.at(max_done, (n + 1) * HG * T))
                    for t in range(T):
                        mm = pe.transpose(m[:, t], nm[n % 2][:, t], w["ident"][:])
                elif name == "ot":
                    pe.wait_ge(pv_out.sem, B.at(pv_out, n + 1))
                    for t in range(T):
                        mm = pe.transpose(m[:, t], oTs[n % 2][:, t], w["ident"][:])
                else:
                    pe.wait_ge(used["ft"].sem, B.at(used["ft"], 1))
                    mm = product(m, w["w1h"][:, n], w["w1l"][:, n], fh, fl)
                mm.then_inc(made[name].sem, 1)

            def wait_bank(B, u, done, banks):
                if u >= banks:
                    pe.wait_ge(done.sem, B.at(done, u - banks + 1))
                elif not isinstance(B.turn, int) or B.number > 0:
                    last = max(v for v in range(UNITS) if v % banks == u % banks)
                    pe.wait_ge(done.sem, B.at(done, last + 1 - UNITS))

            def scores(B, k, j):
                g, u = k // T, k * HG + j
                if k % T == 0 and j == 0:
                    pe.wait_ge(used["nm"].sem, B.at(used["nm"], g + 1))
                wait_bank(B, u, exp_done, ST_BANKS)
                pe.matmul(flat(ST[u % ST_BANKS]), kz[g][:, j, k % T], flat(qm[g % 2]), start=True,
                          stop=True).then_inc(scores_mm.sem, 1)

            def first_scores(B, s, t):
                u = s * T + t
                g, j = u // (HG * T), u // T % HG
                if t == 0 and j == 0:
                    pe.wait_ge(spread[g].sem, B.at(spread[g], 16 * HG))
                    pe.wait_ge(used["qk"].sem, B.at(used["qk"], 2 * g + 2))
                wait_bank(B, u, max_done, MX_BANKS)
                pe.matmul(flat(MX[u % MX_BANKS]), qt[g][:, t], kz[g][:, j].rearrange("p a b -> p (a b)"), start=True,
                          stop=True).then_inc(first_mm.sem, 1)

            def weighted(B, k):
                if not B.exists:
                    return
                g, kt = k // T, k % T
                pe.wait_ge(exp_done.sem, B.at(exp_done, HG * (k + 1)))
                if kt == 0:
                    if g == 0:
                        pe.wait_ge(used["v"].sem, B.at(used["v"], 1))
                    if g > 0 or not isinstance(B.turn, int) or B.number > 0:
                        pe.wait_ge(pv_out.sem, B.at(pv_out, g))
                for j in range(HG):
                    mm = pe.matmul(flat(PV)[32 * j:32 * j + 32], va[B.parity][:, kt, g * HG + j], pr[k % 2][:, j],
                                   start=(kt == 0), stop=(kt == T - 1), skip_group_check=True)
                mm.then_inc(pv_mm.sem, 1)

            def batch_steps(B):
                for k in range(STEPS):
                    C, s = (B, k + AHEAD) if k + AHEAD < STEPS else (B + 1, k + AHEAD - STEPS)
                    for j in range(HG):
                        if B.exists:
                            scores(B, k, j)
                        if C.exists:
                            first_scores(C, s, j)
                        if j == 0:
                            if k == 0:
                                weighted(B + -1, STEPS - 1)
                            else:
                                weighted(B, k - 1)
                        if ("y", -1, 0) in SCHEDULE[k]:
                            mlp_out(B + -1, j)
                        elif j == 1:
                            for name, rel, n in SCHEDULE[k]:
                                small(B + rel, name, n)

            program(pe, batch_steps)


def split(nc, own, raw, high, low):
    own.step(nc.vector.tensor_copy(high, raw))
    own.settle()
    own.step(nc.vector.tensor_tensor(low, raw, high, ALU.subtract))


BACK_WEIGHTS = ("ident", "b1", "b2h", "w2", "lns", "lnsb", "keep", "w1h", "w1l", "qrh", "qrl", "krh", "krl", "wvh",
                "wvl", "minus_half", "eps", "eps_in")


def build_weights(nc, front, back, a):
    w, wanted = {}, {}

    def sb(name, shape, dt=F32):
        wanted[name] = (shape, dt)

    plain = {
        "ident": ([P, P], a["c_ident"]),
        "ramp": ([P, T, E], a["c_ramp"]),
        "heads": ([P, 2, D], a["c_heads"]),
        "wout": ([P, D], a["wout_t"]),
        "bq": ([P, 1], a["bq"]),
        "bkvu": ([P, 3 * D], a["bkvu"]),
        "bout": ([P, T, D], a["bout"]),
        "lnw": ([P, T, D], a["lnw"]),
        "lnb": ([P, T, D], a["lnb"]),
        "b1": ([P, FT], a["b1"]),
        "b2h": ([P, T, D], a["b2"]),
        "w2": ([P, FT, D], a["w2"].rearrange("(n p) d -> p n d", p=P)),
        "lns": ([P, T, D], a["lns"]),
        "lnsb": ([P, T, D], a["lnsb"]),
        "keep": ([P, 5], a["c_keep"]),
    }
    for name, (shape, _) in plain.items():
        sb(name, shape)
    sb("wd", [P, NT, D])
    for name in ("minus_half", "eps", "eps_in"):
        sb(name, [P, T])
    parts = {
        "router": (None, None),
        "wg": [P, NT, P], "wu": [P, NT, P], "wq": [P, P], "wkvu": [P, 3 * D], "w1": [P, FT, P],
        "qr": [P, GRP, P], "kr": [P, GRP, P], "wv": [P, D],
    }
    sb("router", [P, 2 * E], F32R)
    sb("pairs", [2 * E, TE, P], F32R)
    for name, shape in parts.items():
        if name != "router":
            sb(name + "h", shape, F32R)
            sb(name + "l", shape, F32R)
    for name in ("cos_t", "sin_t", "cos_c", "sin_c"):
        sb(name, [P, T, P])
    for scope, keep in ((back, True), (front, False)):
        for name, (shape, dt) in wanted.items():
            if (name in BACK_WEIGHTS) == keep:
                w[name] = scope.enter_context(nc.sbuf_tensor("w_" + name, shape, dt))

    with ExitStack() as tmp:
        def scratch(name, shape, dt=F32):
            return tmp.enter_context(nc.sbuf_tensor("t_" + name, shape, dt))

        raw = {name: scratch(name, shape) for name, shape in parts.items() if name != "router"}
        router = scratch("router", [P, E])
        pairs = scratch("pairs", [2 * E, TE, P])
        theta_t = scratch("theta_t", [P, T, P])
        theta_c = scratch("theta_c", [P, T, P])
        pos_t = scratch("pos_t", [P, T, P])
        pos_c = scratch("pos_c", [P, T, P])
        turns_ = scratch("turns", [P, T, P])
        angle = {(m, f): scratch(f"angle_{m}{f}", [P, T, P]) for m in "tc" for f in ("sin", "cos")}
        loaded = tmp.enter_context(nc.semaphore("w_loaded"))
        angle_ready = tmp.enter_context(nc.semaphore("w_angle"))
        table_ready = tmp.enter_context(nc.semaphore("w_table"))
        dve_own = tmp.enter_context(nc.semaphore("w_dve"))
        block = tmp.enter_context(nc.Block())
        n_loads = [0]

        loads = [(w[n][:], src) for n, (_, src) in plain.items()]
        ge = a["We_gate"].rearrange("(n e) h i -> h n e i", e=2)
        ue = a["We_up"].rearrange("(n e) h i -> h n e i", e=2)
        for n in range(TE):
            loads.append((raw["wg"][:, 1 + n].rearrange("h (e i) -> h e i", e=2), ge[:, n]))
            loads.append((raw["wu"][:, 1 + n].rearrange("h (e i) -> h e i", e=2), ue[:, n]))
        loads += [
            (raw["wg"][:, 0], a["Ws_gate"]), (raw["wu"][:, 0], a["Ws_up"]),
            (w["wd"][:, 0], a["Ws_down"]),
            (w["wd"][:, 1:], a["We_down"].rearrange("(n e) i h -> (e i) n h", e=2)),
            (raw["wq"][:], a["wqkvu_t"][:, 0:D]), (raw["wkvu"][:], a["wqkvu_t"][:, D:]),
            (raw["w1"][:], a["w1"].rearrange("h (n w) -> h n w", n=FT)),
            (raw["qr"][:], a["q_rep"].rearrange("h (g c) -> h g c", g=GRP)),
            (raw["kr"][:], a["k_rep"].rearrange("h (g c) -> h g c", g=GRP)),
            (raw["wv"][:], a["wv"]),
            (router[:], a["gate_t"]), (pairs[:], a["c_pairs"]),
            (theta_t[:], a["theta_t"]), (theta_c[:], a["theta_c"]),
            (pos_t[:], a["c_pos_t"]), (pos_c[:], a["c_pos_c"]),
        ]

        @block.sync
        def _(sp):
            for k, (dst, src) in enumerate(loads):
                sp.dma_start(dst, src).then_inc(loaded, 16)

        @block.vector
        def _(dve):
            own = Chain(dve, dve_own, 0)
            own.step(nc.vector.memset(w["minus_half"][:], -0.5))
            own.step(nc.vector.memset(w["eps"][:], EPS))
            own.step(nc.vector.memset(w["eps_in"][:], EPS_IN))
            dve.wait_ge(loaded, 16 * len(loads))
            for name in raw:
                split(nc, own, raw[name][:], w[name + "h"][:], w[name + "l"][:])
            split(nc, own, router[:], w["router"][:, 0:E], w["router"][:, E:2 * E])
            own.step(nc.vector.tensor_copy(w["pairs"][:], pairs[:]))
            own.step(nc.vector.tensor_scalar(w["b2h"][:], w["b2h"][:], 0.5, None, ALU.mult))
            for m, theta, pos in (("t", theta_t, pos_t), ("c", theta_c, pos_c)):
                own.step(nc.vector.tensor_tensor(theta[:], theta[:], pos[:], ALU.mult))
                for f, quarter in (("sin", 0.0), ("cos", 0.25)):
                    own.settle()
                    own.step(nc.vector.tensor_scalar(turns_[:], theta[:], float(1 / (2 * np.pi)), quarter,
                                                     ALU.mult, ALU.add))
                    own.settle()
                    own.step(nc.vector.tensor_scalar(turns_[:], turns_[:], BIG_ROUND, None, ALU.add))
                    own.settle()
                    own.step(nc.vector.tensor_scalar(turns_[:], turns_[:], -BIG_ROUND, None, ALU.add))
                    r = angle[m, f]
                    src = theta
                    for part in TWO_PI:
                        own.settle()
                        own.step(nc.vector.scalar_tensor_tensor(out=r[:], in0=turns_[:], scalar=-part, in1=src[:],
                                                                op0=ALU.mult, op1=ALU.add))
                        src = r
                    own.settle()
                    own.step(nc.vector.tensor_scalar(r[:], r[:], float(quarter * 2 * np.pi), PI_32,
                                                     ALU.add, ALU.min))
                    own.settle()
                    nc.vector.tensor_scalar(r[:], r[:], -PI_32, None, ALU.max).then_inc(angle_ready, 1)

        @block.scalar
        def _(act):
            n = 0
            for m in "tc":
                for f in ("sin", "cos"):
                    n += 1
                    act.wait_ge(angle_ready, n)
                    nc.scalar.activation(w[f"{f}_{m}"][:], angle[m, f][:], ACT.Sin).then_inc(table_ready, 1)
    return w


def lay_out(inputs):
    f = np.float32

    def rows(v, n=T):
        v = np.asarray(v).reshape(-1)
        return np.ascontiguousarray(np.broadcast_to(v, (P, n) + v.shape))

    wq, wk = np.asarray(inputs["L1_attn_wq"]), np.asarray(inputs["L1_attn_wk"])
    q_rep, k_rep = np.zeros((D, GRP, HG, 4, DH), f), np.zeros((D, GRP, HG, 4, DH), f)
    for part in range(3):
        q_rep[:, :, :, part] = wq.reshape(D, GRP, HG, DH)
        k_rep[:, :, :, part] = wk.reshape(D, GRP, HG, DH)
    tok = np.arange(P)
    pos = (T * tok[:, None] + np.arange(T)[None, :]).astype(f)
    theta = np.asarray(inputs["L0_attn_theta"]).reshape(D)
    bias = np.asarray(inputs["L0_attn_bqkvu"])
    keep = np.zeros((P, 5), f)
    r = np.arange(P) % 32
    part = r // DH
    keep[:, 0] = np.where(part == 1, -1, 1)
    keep[:, 1] = part == 1
    keep[:, 2] = np.where(part == 2, -1, 1)
    keep[:, 3] = part == 2
    keep[:, 4] = r == MAX_ROW
    head = np.arange(P) // DH
    return {
        "x": np.asarray(inputs["L0_attn_x"]),
        "We_gate": inputs["L0_ffn_We_gate"], "We_up": inputs["L0_ffn_We_up"], "We_down": inputs["L0_ffn_We_down"],
        "Ws_gate": inputs["L0_ffn_Ws_gate"], "Ws_up": inputs["L0_ffn_Ws_up"], "Ws_down": inputs["L0_ffn_Ws_down"],
        "gate_t": np.asarray(inputs["L0_ffn_gate_weight"]).T,
        "wqkvu_t": np.asarray(inputs["L0_attn_Wqkvu"]).T,
        "wout_t": np.asarray(inputs["L0_attn_Wout"]).T,
        "bq": bias[:D, None], "bkvu": rows(bias[D:], 1)[:, 0], "bout": rows(inputs["L0_attn_bout"]),
        "lnw": rows(inputs["L0_attn_ln_w"]), "lnb": rows(inputs["L0_attn_ln_b"]),
        "w1": inputs["L1_ffn_w1"], "w2": inputs["L1_ffn_w2"],
        "b1": np.asarray(inputs["L1_ffn_b1"]).reshape(FT, P).T, "b2": rows(inputs["L1_ffn_b2"]),
        "lns": rows(inputs["L1_attn_ln_scale"]), "lnsb": rows(inputs["L1_attn_ln_bias"]),
        "wv": inputs["L1_attn_wv"],
        "q_rep": q_rep.reshape(D, GRP * P), "k_rep": k_rep.reshape(D, GRP * P),
        "theta_t": rows(theta), "theta_c": np.broadcast_to(theta[:, None, None], (P, T, P)),
        "c_pos_t": np.broadcast_to(pos[:, :, None], (P, T, P)), "c_pos_c": np.broadcast_to(pos.T[None], (P, T, P)),
        "c_ident": np.eye(P, dtype=f),
        "c_ramp": np.broadcast_to(np.arange(E, 0, -1, dtype=f), (P, T, E)),
        "c_heads": np.broadcast_to((head[:, None] == head[None, :]).astype(f)[:, None], (P, 2, D)),
        "c_pairs": (np.arange(2 * E)[:, None, None] % E == 2 * np.arange(TE)[None, :, None]
                    + (np.arange(P) // I_E)[None, None, :]).astype(f),
        "c_keep": keep,
    }


def kernel(**inputs):
    import concourse.bacc as bacc
    from concourse.bass_utils import run_bass_kernel_spmd

    nc = bacc.Bacc("TRN2", target_bir_lowering=False, num_devices=1)
    arrays, args = {}, {}
    for name, a in lay_out(inputs).items():
        a = np.ascontiguousarray(a)
        arrays[f"in_{name}"] = a
        args[name] = nc.dram_tensor(f"in_{name}", a.shape, mybir.dt.from_np(a.dtype), kind="ExternalInput").ap()
    shape = arrays["in_x"].shape
    assert shape == (NB, N, D)
    mid = nc.dram_tensor("mid", shape, F32, kind="Internal").ap()
    out = nc.dram_tensor("out", shape, F32, kind="ExternalOutput").ap()
    with ExitStack() as back:
        with ExitStack() as front:
            w = build_weights(nc, front, back, args)
            build_front(nc, w, args["x"], mid, args["c_ident"], NB // 2)
        build_back(nc, w, mid, out, NB)
    r = run_bass_kernel_spmd(nc, [arrays], core_ids=[0])
    return r.results[0]["out"]
```

```python
from contextlib import ExitStack

import numpy as np

import concourse.bass as bass
from concourse import mybir

F32 = mybir.dt.float32
F32R = mybir.dt.float32r
ALU = mybir.AluOpType
ACT = mybir.ActivationFunctionType
AX = mybir.AxisListType

P = 128
NB = 16
N = 512
T = N // P
D = 128
H, DH = 16, 8
E = 16
I_E = 64
TE = E * I_E // P
NT = TE + 1
FT = 4
GRP = 4
HG = H // GRP
EPS = 1e-5
EPS_IN = 1e-6
SM_SCALE = float(D) ** -0.5
BIG_ROUND = 12582912.0
TWO_PI = (6.28125, 0.0019350051879882812, 3.020991e-07)
PI_32 = 3.1415925


class Signal:

    def __init__(self, sem, per, pre=0):
        self.sem, self.per, self.pre = sem, per, pre

    def at(self, i, n):
        return i * self.per + (self.pre + n)


class Chain:

    def __init__(self, eng, sem, per):
        self.eng, self.sem, self.per = eng, sem, per
        self.base, self.n = 0, 0

    def enter(self, turn):
        self.outside = self.base + self.n
        self.base, self.n = turn * self.per + self.outside, 0

    def leave(self, turns):
        assert self.n == self.per, f"chain: {self.n} steps in a turn, {self.per} declared"
        self.base, self.n = self.outside + turns * self.per, 0

    def step(self, ins):
        ins.then_inc(self.sem, 1)
        self.n += 1

    def settle(self, but=0):
        self.eng.wait_ge(self.sem, self.base + (self.n - but))


MAX_ROW = 3 * DH

ATT, MLP = "att", "mlp"
SIDE = [ATT, MLP, ATT, MLP]
SIDE_BATCH = [0, 1, 1, 0]
MAIN_BATCH = [1, 1, 0, 0]
NM = len(SIDE)
N_ATT, N_MLP = SIDE.count(ATT), SIDE.count(MLP)
DVE_STEPS = 2 * NM + 21 * NM + N_ATT
POOL_STEPS = 3 * NM + 5 * N_ATT
PAD = 2


PREPARE = {
    MLP: {"statistics": 0, "transpose": 2, "low": 2, "logits": 3, "first": 4, "second": 5, "weights": 6},
    ATT: {"statistics": 1, "transpose": 3, "low": 4, "logits": 5, "first": 6, "second": 7, "weights": 8},
}


def nth(m):
    return SIDE[:m].count(SIDE[m])


def build_front(nc, weights, x_dram, mid_dram, ident_dram, turns):
    w = weights
    with ExitStack() as ctx:
        def sb(name, shape, dt=F32):
            return ctx.enter_context(nc.sbuf_tensor(name, shape, dt))

        def ps(name, shape):
            return ctx.enter_context(nc.psum_tensor(name, shape, F32))

        def sig(name, per, pre=0):
            return Signal(ctx.enter_context(nc.semaphore(name)), per, pre)

        xin = [sb(f"xin{p}", [P, T, D]) for p in range(2)]
        xw = [sb(f"xw{p}", [P, T, D]) for p in range(2)]
        xo = [sb(f"xo{p}", [P, T, D]) for p in range(2)]
        z = sb("z", [P, T, D])
        xh = [sb(f"xh{p}", [P, T, P], F32R) for p in range(2)]
        xl = [sb(f"xl{p}", [P, T, P], F32R) for p in range(2)]
        stats = sb("stats", [P, T, 6])
        mv = sb("mv", [P, T, 2])
        vpe = sb("vpe", [P, T])
        rstd = sb("rstd", [P, T, 1])
        zs = sb("zs", [P, T, D])
        xhs = sb("xhs", [P, T, P], F32R)
        xls = sb("xls", [P, T, P], F32R)
        stats_s = sb("stats_s", [P, T, 6])
        mv_s = sb("mv_s", [P, T, 2])
        vpe_s = sb("vpe_s", [P, T])
        rstd_s = sb("rstd_s", [P, T])
        xb = sb("xb", [P, T, D])
        nudge = sb("nudge", [P, 1])
        lb = sb("lb", [P, T, E])
        lg = sb("lg", [P, T, E])
        en = sb("en", [P, T, E])
        sc = sb("sc", [P, T, E])
        hit = sb("hit", [P, T, E])
        first = sb("first", [P, T, E])
        second = sb("second", [P, T, E])
        rest = sb("rest", [P, T, E])
        share = sb("share", [P, T, E])
        m1 = sb("m1", [P, T, 1])
        m2 = sb("m2", [P, T, 1])
        r1 = sb("r1", [P, T, 1])
        den = sb("den", [P, T, 1])
        comb = sb("comb", [P, T, E])
        comb2 = sb("comb2", [P, T, 2 * E])
        combh = sb("combh", [P, T, E], F32R)
        cT = [sb(f"cT{p}", [2 * E, T, P], F32R) for p in range(2)]
        sbuf_s = [sb(f"s{p}", [P, T, P]) for p in range(2)]
        su = [sb(f"su{k}", [P, T, P]) for k in range(2)]
        h = [sb(f"h{k}", [P, T, P]) for k in range(3)]
        kvu = sb("kvu", [P, T, 3 * D])
        kc = sb("kc", [P, 2, T, D])
        qa = sb("qa", [P, T, P])
        qc = sb("qc", [P, 2, T, P])
        kvm = sb("kvm", [P, 2, D])
        uw = sb("uw", [P, T, D])
        ub = sb("ub", [P, T, D])
        stats2 = sb("stats2", [P, T, 6])
        mv2 = sb("mv2", [P, T, 2])
        vpe2 = sb("vpe2", [P, T])
        rstd2 = sb("rstd2", [P, T])
        on = sb("on", [P, T, D])
        og = sb("og", [P, T, D])
        oT = sb("oT", [P, T, P])
        hs = [sb(f"hs{k}", [P, T, P]) for k in range(2)]

        G = [ps(f"G{k}", [P, T, P]) for k in range(2)]
        U = ps("U", [P, T, P])
        C = ps("C", [P, T, P])
        Y = ps("Y", [P, T, P])
        Z = ps("Z", [P, T, P])
        S = [ps(f"S{k}", [P, T, P]) for k in range(2)]

        x_loaded = [sig(f"x_loaded{p}", 16) for p in range(2)]
        stored = [sig(f"stored{p}", 16, 16) for p in range(2)]
        mv_ready = sig("mv_ready", NM, 1)
        rstd_ready = sig("rstd_ready", NM, 1)
        z_ready = sig("z_ready", NM, 1)
        zT_ready = sig("zT_ready", NM, 1)
        xh_ready = sig("xh_ready", NM, 1)
        xl_ready = sig("xl_ready", NM, 1)
        logits_ready = sig("logits_ready", NM, 1)
        lb_ready = sig("lb_ready", NM, 1)
        lg_ready = sig("lg_ready", NM, 1)
        score_ready = sig("score_ready", NM, 1)
        comb_ready = sig("comb_ready", NM, 1)
        combT_ready = sig("combT_ready", NM, 1)
        cT_ready = sig("cT_ready", NM, 1)
        gate_ready = sig("gate_ready", NT * NM, NT)
        act_done = sig("act_done", NT * NM, NT)
        up_ready = sig("up_ready", NT * NM, NT)
        up_used = sig("up_used", NT * NM, NT)
        weight_ready = sig("weight_ready", TE * NM, TE)
        h_ready = sig("h_ready", TE * NM, TE)
        down_done = sig("down_done", NT * NM, NT)
        main_done = sig("main_done", NM, 2)
        side_done = sig("side_done", NM, 1)
        smv_ready = sig("smv_ready", NM)
        srstd_ready = sig("srstd_ready", NM)
        sz_ready = sig("sz_ready", NM)
        szT_ready = sig("szT_ready", NM)
        xhs_ready = sig("xhs_ready", NM)
        xls_ready = sig("xls_ready", NM)
        xb_ready = sig("xb_ready", NM)
        side_mm = sig("side_mm", NM)
        hid_mm = sig("hid_mm", FT * N_MLP)
        hid_ready = sig("hid_ready", FT * N_MLP)
        q_mm = sig("q_mm", N_ATT)
        kvu_mm = sig("kvu_mm", T * N_ATT)
        kvu_out = sig("kvu_out", T * N_ATT)
        qa_ready = sig("qa_ready", N_ATT)
        ka_ready = sig("ka_ready", N_ATT)
        qc_ready = sig("qc_ready", N_ATT)
        kc_ready = sig("kc_ready", N_ATT)
        ks_ready = sig("ks_ready", N_ATT)
        on_ready = sig("on_ready", N_ATT)
        kv_mm = sig("kv_mm", N_ATT)
        kvm_ready = sig("kvm_ready", N_ATT)
        o_mm = sig("o_mm", N_ATT)
        mv2_ready = sig("mv2_ready", N_ATT)
        rstd2_ready = sig("rstd2_ready", N_ATT)
        og_ready = sig("og_ready", N_ATT)
        oT_mm = sig("oT_mm", N_ATT)
        oT_ready = sig("oT_ready", N_ATT)
        dve_own = ctx.enter_context(nc.semaphore("dve_own"))
        pool_own = ctx.enter_context(nc.semaphore("pool_own"))

        xd = x_dram.rearrange("b (p t) d -> b p t d", p=P)
        md = mid_dram.rearrange("b (p t) d -> b p t d", p=P)
        block = ctx.enter_context(nc.Block())

        def source(q):
            b = MAIN_BATCH[q % NM]
            return xin[b] if q % 2 == 1 else xw[b]

        @block.sync
        def _(sp):
            for p in range(2):
                sp.dma_start(xin[p][:], xd[p]).then_inc(x_loaded[p].sem, 16)
            for p in range(2):
                sp.dma_start(xo[p][:, 0, :], ident_dram).then_inc(stored[p].sem, 16)

            def store(i, m):
                p = SIDE_BATCH[m]
                sp.wait_ge(side_done.sem, side_done.at(i, m + 1))
                sp.dma_start(md[i * 2 + (PAD - p)], xo[p][:]).then_inc(stored[p].sem, 16)

            def load(i, m, batch):
                p = MAIN_BATCH[m]
                sp.wait_ge(main_done.sem, main_done.at(i, m + 1))
                sp.dma_start(xin[p][:], xd[batch]).then_inc(x_loaded[p].sem, 16)

            load(0, -1, 2)
            if turns > 2:
                with sp.Fori(0, turns - 2) as i:
                    store(i, 1)
                    load(i, 1, i * 2 + 3)
                    store(i, 3)
                    load(i, 3, i * 2 + 4)
            store(turns - 2, 1)
            load(turns - 2, 1, 2 * turns - 1)
            store(turns - 2, 3)
            load(turns - 2, 3, 2 * turns - 2)
            store(turns - 1, 1)
            store(turns - 1, 3)
            sp.wait_ge(side_done.sem, side_done.at(turns, 1))
            sp.dma_start(md[2 * turns - 1 + PAD], xo[1][:]).then_inc(stored[1].sem, 16)
            for p in range(2):
                sp.wait_ge(x_loaded[p].sem, 16 * (turns + 1 - p))
                sp.wait_ge(stored[p].sem, 16 * (turns + 1 + p))

        @block.gpsimd
        def _(pool):
            own = Chain(pool, pool_own, POOL_STEPS)

            def rsqrt(out, tmp, mean_var, ready, value, done):
                pool.wait_ge(ready.sem, value)
                own.step(nc.gpsimd.tensor_tensor(tmp[:], mean_var[:, :, 1], w["eps"][:], ALU.add))
                own.settle()
                nc.gpsimd.tensor_tensor(out, tmp[:], w["minus_half"][:], ALU.pow).then_inc(done.sem, 1)

            def main_normalise(q, i):
                rsqrt(rstd[:, :, 0], vpe, mv, mv_ready, mv_ready.at(i, q + 1), rstd_ready)
                pool.wait_ge(rstd_ready.sem, rstd_ready.at(i, q + 1))
                own.step(nc.gpsimd.tensor_tensor(z[:], source(q)[:], mv[:, :, 0:1].broadcast_to([P, T, D]),
                                                 ALU.subtract))
                own.settle()
                nc.gpsimd.tensor_tensor(z[:], z[:], rstd[:].broadcast_to([P, T, D]), ALU.mult).then_inc(z_ready.sem, 1)

            def side_start(m, i, k):
                rsqrt(rstd_s[:], vpe_s, mv_s, smv_ready, smv_ready.at(i, k + 1), srstd_ready)
                pool.wait_ge(side_done.sem, side_done.at(i, k))
                bias = w["bout"] if SIDE[m] == ATT else w["b2h"]
                nc.gpsimd.tensor_tensor(xb[:], xw[SIDE_BATCH[m]][:], bias[:], ALU.add).then_inc(xb_ready.sem, 1)

            main_normalise(-1, 0)
            main_normalise(0, 0)
            with pool.Fori(0, turns) as i:
                own.enter(i)
                for m in range(NM):
                    side_start(m, i, m)
                    main_normalise(m + 1, i)
                    if SIDE[m] == ATT:
                        a = nth(m)
                        pool.wait_ge(ka_ready.sem, ka_ready.at(i, a + 1))
                        nc.gpsimd.tensor_tensor(kc[:, 1], kvu[:, :, 0:D], w["sin_t"][:],
                                                ALU.mult).then_inc(ks_ready.sem, 1)
                        pool.wait_ge(qa_ready.sem, qa_ready.at(i, a + 1))
                        own.step(nc.gpsimd.tensor_tensor(qc[:, 0], qa[:], w["cos_c"][:], ALU.mult))
                        nc.gpsimd.tensor_tensor(qc[:, 1], qa[:], w["sin_c"][:], ALU.mult).then_inc(qc_ready.sem, 1)
                        pool.wait_ge(kvu_out.sem, kvu_out.at(i, T * (a + 1)))
                        own.step(nc.gpsimd.tensor_tensor(uw[:], kvu[:, :, 2 * D:], w["lnw"][:], ALU.mult))
                        own.step(nc.gpsimd.tensor_tensor(ub[:], kvu[:, :, 2 * D:], w["lnb"][:], ALU.mult))
                        rsqrt(rstd2[:], vpe2, mv2, mv2_ready, mv2_ready.at(i, a + 1), rstd2_ready)
                        pool.wait_ge(on_ready.sem, on_ready.at(i, a + 1))
                        own.step(nc.gpsimd.tensor_tensor(og[:], on[:], uw[:], ALU.mult))
                        own.settle()
                        nc.gpsimd.tensor_tensor(og[:], og[:], ub[:], ALU.add).then_inc(og_ready.sem, 1)
                own.leave(turns)
            side_start(1, turns, 0)

        @block.scalar
        def _(act):
            def main_high(q, i):
                act.wait_ge(zT_ready.sem, zT_ready.at(i, q + 1))
                nc.scalar.activation(xh[q % 2][:], Z[:], ACT.Copy).then_inc(xh_ready.sem, 1)

            def logits_half(q, i):
                act.wait_ge(logits_ready.sem, logits_ready.at(i, q + 1))
                nc.scalar.activation(lb[:], Z[:, :, E:2 * E], ACT.Copy).then_inc(lb_ready.sem, 1)

            def scores(q, i):
                act.wait_ge(lg_ready.sem, lg_ready.at(i, q + 1))
                nc.scalar.activation(en[:], lg[:], ACT.Exp, scale=-1.0).then_inc(score_ready.sem, 1)

            def side_high(i, k):
                act.wait_ge(szT_ready.sem, szT_ready.at(i, k + 1))
                nc.scalar.activation(xhs[:], S[0][:], ACT.Copy).then_inc(xhs_ready.sem, 1)

            def hidden(m, k, i):
                act.wait_ge(hid_mm.sem, hid_mm.at(i, FT * nth(m) + k + 1))
                nc.scalar.activation(hs[k % 2][:], S[1][:], ACT.Relu,
                                     bias=w["b1"][:, k:k + 1]).then_inc(hid_ready.sem, 1)

            def slot(m, i, side, prepare):
                g0, steps = NT * m, PREPARE[side or MLP]
                for n in range(NT):
                    act.wait_ge(gate_ready.sem, gate_ready.at(i, g0 + n + 1))
                    if n >= 2:
                        act.wait_ge(up_used.sem, up_used.at(i, g0 + n - 1))
                    nc.scalar.activation(sbuf_s[n % 2][:], G[n % 2][:], ACT.Silu).then_inc(act_done.sem, 1)
                    if n == 0:
                        act.wait_ge(combT_ready.sem, combT_ready.at(i, m + 1))
                        nc.scalar.activation(cT[m % 2][:], Z[0:2 * E], ACT.Copy).then_inc(cT_ready.sem, 1)
                    if n == 1 and side:
                        side_high(i, m)
                    if side == ATT:
                        a = nth(m)
                        if n == 3:
                            act.wait_ge(kvu_out.sem, kvu_out.at(i, T * (a + 1)))
                            nc.scalar.activation(kvu[:, :, 0:D], kvu[:, :, 0:D], ACT.Silu).then_inc(ka_ready.sem, 1)
                            act.wait_ge(q_mm.sem, q_mm.at(i, a + 1))
                            nc.scalar.activation(qa[:], S[1][:], ACT.Silu, bias=w["bq"][:]).then_inc(qa_ready.sem, 1)
                        if n == 8:
                            act.wait_ge(oT_mm.sem, oT_mm.at(i, a + 1))
                            nc.scalar.activation(oT[:], S[0][:], ACT.Copy).then_inc(oT_ready.sem, 1)
                    elif side == MLP:
                        if 2 <= n < 2 + FT:
                            hidden(m, n - 2, i)
                    if prepare:
                        if n == steps["transpose"]:
                            main_high(m + 1, i)
                        if n == steps["logits"]:
                            logits_half(m + 1, i)
                        if n == steps["logits"] + 1:
                            scores(m + 1, i)

            main_high(-1, 0)
            logits_half(-1, 0)
            scores(-1, 0)
            slot(-1, 0, None, True)
            with act.Fori(0, turns) as i:
                for m in range(NM):
                    slot(m, i, SIDE[m], True)
            slot(0, turns, None, False)
            side_high(turns, 0)
            for k in range(FT):
                hidden(1, k, turns)

        @block.vector
        def _(dve):
            own = Chain(dve, dve_own, DVE_STEPS)

            def step(ins):
                own.step(ins)

            def statistics(src, st, m, done):
                for t in range(T):
                    ins = nc.vector.bn_stats(st[:, t], src[:, t])
                step(ins)
                own.settle()
                nc.vector.memset(nudge[:], 0.0)
                for t in range(T):
                    ins = nc.vector.bn_aggr(m[:, t], st[:, t])
                ins.then_inc(done.sem, 1)

            def normalise(out, src, m, r):
                for t in range(T):
                    ins = nc.vector.tensor_scalar(out[:, t], src[:, t], m[:, t, 0:1], r[:, t:t + 1],
                                                  ALU.subtract, ALU.mult)
                return ins

            def main_stats(q, i):
                if q % 2 == 1:
                    p = MAIN_BATCH[q]
                    dve.wait_ge(x_loaded[p].sem, x_loaded[p].at(i, 32 if q == 3 else 16))
                elif q == 0:
                    dve.wait_ge(main_done.sem, main_done.at(i, -1))
                else:
                    dve.wait_ge(side_done.sem, side_done.at(i, q - 1))
                statistics(source(q), stats, mv, mv_ready)

            def main_low(q, i):
                dve.wait_ge(xh_ready.sem, xh_ready.at(i, q + 1))
                nc.vector.tensor_tensor(xl[q % 2][:], Z[:], xh[q % 2][:], ALU.subtract).then_inc(xl_ready.sem, 1)

            def logits(q, i):
                dve.wait_ge(lb_ready.sem, lb_ready.at(i, q + 1))
                nc.vector.tensor_tensor(lg[:], Z[:, :, 0:E], lb[:], ALU.add).then_inc(lg_ready.sem, 1)

            def wide(t):
                return t[:].broadcast_to([P, T, E])

            def routing_first(q, i):
                dve.wait_ge(score_ready.sem, score_ready.at(i, q + 1))
                step(nc.vector.tensor_scalar(en[:], en[:], 1.0, None, ALU.add))
                own.settle()
                step(nc.vector.reciprocal(sc[:], en[:]))
                own.settle()
                step(nc.vector.tensor_reduce(m1[:], sc[:], AX.X, ALU.max))
                own.settle()
                step(nc.vector.tensor_tensor(hit[:], sc[:], wide(m1), ALU.is_equal))
                own.settle()
                step(nc.vector.tensor_tensor(hit[:], hit[:], w["ramp"][:], ALU.mult))
                own.settle()
                step(nc.vector.tensor_reduce(r1[:], hit[:], AX.X, ALU.max))
                own.settle()
                step(nc.vector.tensor_tensor(first[:], hit[:], wide(r1), ALU.is_equal))

            def routing_second(q, i):
                own.settle()
                step(nc.vector.scalar_tensor_tensor(out=rest[:], in0=first[:], scalar=-2.0, in1=sc[:],
                                                    op0=ALU.mult, op1=ALU.add))
                own.settle()
                step(nc.vector.tensor_reduce(m2[:], rest[:], AX.X, ALU.max))
                own.settle()
                step(nc.vector.tensor_tensor(hit[:], rest[:], wide(m2), ALU.is_equal))
                step(nc.vector.tensor_tensor(den[:], m1[:], m2[:], ALU.add))
                own.settle(1)
                step(nc.vector.tensor_tensor(hit[:], hit[:], w["ramp"][:], ALU.mult))
                own.settle(1)
                step(nc.vector.tensor_scalar(den[:], den[:], 1e-20, None, ALU.add))
                own.settle(1)
                step(nc.vector.tensor_reduce(r1[:], hit[:], AX.X, ALU.max))
                own.settle(1)
                step(nc.vector.reciprocal(den[:], den[:]))
                own.settle(1)
                step(nc.vector.tensor_tensor(second[:], hit[:], wide(r1), ALU.is_equal))
                own.settle(1)
                step(nc.vector.tensor_tensor(share[:], sc[:], wide(den), ALU.mult))

            def routing_weights(q, i):
                own.settle(1)
                step(nc.vector.tensor_tensor(first[:], first[:], second[:], ALU.add))
                own.settle()
                step(nc.vector.tensor_tensor(comb[:], first[:], share[:], ALU.mult))
                own.settle()
                step(nc.vector.tensor_copy(combh[:], comb[:]))
                own.settle()
                step(nc.vector.tensor_copy(comb2[:, :, 0:E], combh[:]))
                nc.vector.tensor_tensor(comb2[:, :, E:2 * E], comb[:], combh[:],
                                        ALU.subtract).then_inc(comb_ready.sem, 1)

            def activated(m, n, i):
                g0, c0 = NT * m, TE * m
                dve.wait_ge(act_done.sem, act_done.at(i, g0 + n + 1))
                dve.wait_ge(up_ready.sem, up_ready.at(i, g0 + n + 1))
                if n >= 3:
                    dve.wait_ge(h_ready.sem, h_ready.at(i, c0 + n - 2))
                elif c0 + n > 2:
                    dve.wait_ge(h_ready.sem, h_ready.at(i, c0))
                out = h[0] if n == 0 else su[n % 2]
                nc.vector.tensor_tensor(out[:], U[:], sbuf_s[n % 2][:], ALU.mult).then_inc(up_used.sem, 1)

            def routed(m, n, i):
                g0, c0 = NT * m, TE * m
                dve.wait_ge(up_used.sem, up_used.at(i, g0 + n + 1))
                dve.wait_ge(weight_ready.sem, weight_ready.at(i, c0 + n))
                if n >= 3:
                    dve.wait_ge(down_done.sem, down_done.at(i, g0 + n - 2))
                nc.vector.tensor_tensor(h[n % 3][:], C[:], su[n % 2][:], ALU.mult).then_inc(h_ready.sem, 1)

            def main_residual(m, i):
                dve.wait_ge(down_done.sem, down_done.at(i, NT * (m + 1)))
                nc.vector.scalar_tensor_tensor(out=xw[MAIN_BATCH[m]][:], in0=Y[:], scalar=0.5, in1=source(m)[:],
                                               op0=ALU.mult, op1=ALU.add).then_inc(main_done.sem, 1)

            def side_stats(m, i, k):
                dve.wait_ge(main_done.sem, main_done.at(i, m))
                statistics(xw[SIDE_BATCH[m]], stats_s, mv_s, smv_ready)

            def side_normalise(m, i, k):
                dve.wait_ge(srstd_ready.sem, srstd_ready.at(i, k + 1))
                normalise(zs, xw[SIDE_BATCH[m]], mv_s, rstd_s).then_inc(sz_ready.sem, 1)

            def side_low(i, k):
                dve.wait_ge(xhs_ready.sem, xhs_ready.at(i, k + 1))
                nc.vector.tensor_tensor(xls[:], S[0][:], xhs[:], ALU.subtract).then_inc(xls_ready.sem, 1)

            def side_residual(m, i, k):
                p = SIDE_BATCH[m]
                dve.wait_ge(side_mm.sem, side_mm.at(i, k + 1))
                dve.wait_ge(xb_ready.sem, xb_ready.at(i, k + 1))
                if SIDE[m] == ATT:
                    ins = nc.vector.tensor_tensor(xw[p][:], S[1][:], xb[:], ALU.add)
                else:
                    dve.wait_ge(stored[p].sem, stored[p].at(i, 0))
                    ins = nc.vector.scalar_tensor_tensor(out=xo[p][:], in0=S[0][:], scalar=0.5, in1=xb[:],
                                                         op0=ALU.mult, op1=ALU.add)
                ins.then_inc(side_done.sem, 1)

            def kvu_bias(a, ts, i):
                for t in ts:
                    dve.wait_ge(kvu_mm.sem, kvu_mm.at(i, T * a + t + 1))
                    nc.vector.tensor_tensor(kvu[:, t], S[1 - t % 2][:].rearrange("p a b -> p (a b)")[:, 0:3 * D],
                                            w["bkvu"][:], ALU.add).then_inc(kvu_out.sem, 1)

            def turn_keys(a, i):
                dve.wait_ge(ka_ready.sem, ka_ready.at(i, a + 1))
                nc.vector.tensor_tensor(kc[:, 0], kvu[:, :, 0:D], w["cos_t"][:], ALU.mult).then_inc(kc_ready.sem, 1)

            def mask_heads(a, i):
                dve.wait_ge(kv_mm.sem, kv_mm.at(i, a + 1))
                nc.vector.tensor_tensor(kvm[:], S[0][:, 0:2], w["heads"][:], ALU.mult).then_inc(kvm_ready.sem, 1)

            def out_stats(a, i):
                dve.wait_ge(o_mm.sem, o_mm.at(i, a + 1))
                statistics(S[1], stats2, mv2, mv2_ready)

            def out_normalise(a, i):
                dve.wait_ge(rstd2_ready.sem, rstd2_ready.at(i, a + 1))
                normalise(on, S[1], mv2, rstd2).then_inc(on_ready.sem, 1)

            def slot(m, i, side, prepare):
                a, steps = nth(m), PREPARE[side or MLP]
                if side:
                    side_stats(m, i, m)
                for n in range(NT):
                    if side == ATT and n == 5:
                        mask_heads(a, i)
                    activated(m, n, i)
                    if n > 0:
                        routed(m, n, i)
                    if side:
                        if n == 0:
                            side_normalise(m, i, m)
                        if n == 1:
                            side_low(i, m)
                    if side == ATT:
                        if n == 2:
                            kvu_bias(a, (0, 1), i)
                        if n == 3:
                            kvu_bias(a, (2, 3), i)
                            turn_keys(a, i)
                        if n == 5:
                            out_stats(a, i)
                        if n == 6:
                            out_normalise(a, i)
                        if n == 8:
                            side_residual(m, i, m)
                    if side == MLP and n == 7:
                        side_residual(m, i, m)
                    if prepare:
                        if n == steps["statistics"]:
                            main_stats(m + 1, i)
                        if n == steps["low"]:
                            main_low(m + 1, i)
                        if n == steps["logits"]:
                            logits(m + 1, i)
                        if n == steps["first"]:
                            routing_first(m + 1, i)
                        if n == steps["second"]:
                            routing_second(m + 1, i)
                        if n == steps["weights"]:
                            routing_weights(m + 1, i)
                main_residual(m, i)

            nc.vector.memset(xw[1][:], 0.0).then_inc(main_done.sem, 1)
            nc.vector.memset(nudge[:], 0.0).then_inc(side_done.sem, 1)
            for f in (main_stats, main_low, logits, routing_first, routing_second, routing_weights):
                f(-1, 0)
            slot(-1, 0, None, True)
            with dve.Fori(0, turns) as i:
                own.enter(i)
                for m in range(NM):
                    slot(m, i, SIDE[m], True)
                own.leave(turns)
            slot(0, turns, None, False)
            side_stats(1, turns, 0)
            side_normalise(1, turns, 0)
            side_low(turns, 0)
            side_residual(1, turns, 0)

        @block.tensor
        def _(pe):
            def flat(t):
                return t[:].rearrange("p a b -> p (a b)")

            def main_transposes(q, i):
                pe.wait_ge(z_ready.sem, z_ready.at(i, q + 1))
                for t in range(T):
                    mm = pe.transpose(Z[:, t], z[:, t], w["ident"][:])
                mm.then_inc(zT_ready.sem, 1)

            def logits(q, i):
                pe.wait_ge(xl_ready.sem, xl_ready.at(i, q + 1))
                for t in range(T):
                    pe.matmul(Z[:, t, 0:2 * E], xh[q % 2][:, t], w["router"][:], start=True, stop=False,
                              skip_group_check=True)
                    mm = pe.matmul(Z[:, t, 0:2 * E], xl[q % 2][:, t], w["router"][:], start=False, stop=True,
                                   skip_group_check=True)
                mm.then_inc(logits_ready.sem, 1)

            def product(bank, wh, wl, high, low):
                pe.matmul(flat(bank), wh, flat(high), start=True, stop=False)
                pe.matmul(flat(bank), wl, flat(high), start=False, stop=False)
                return pe.matmul(flat(bank), wh, flat(low), start=False, stop=True)

            def down(bank, hid, wd, first):
                for t in range(T):
                    mm = pe.matmul(bank[:, t], hid[:, t], wd, start=(first and t == 0), stop=True,
                                   skip_group_check=True)
                return mm

            def moe_down(m, n, i):
                if n == 0:
                    pe.wait_ge(main_done.sem, main_done.at(i, m))
                    pe.wait_ge(up_used.sem, up_used.at(i, NT * m + 1))
                else:
                    pe.wait_ge(h_ready.sem, h_ready.at(i, TE * m + n))
                down(Y, h[n % 3], w["wd"][:, n], n == 0).then_inc(down_done.sem, 1)

            def comb_transposes(m, i):
                pe.wait_ge(comb_ready.sem, comb_ready.at(i, m + 1))
                for t in range(T):
                    mm = pe.transpose(Z[0:2 * E, t], comb2[:, t], w["ident"][:])
                mm.then_inc(combT_ready.sem, 1)

            def routing_weights(m, n, i):
                if n == 1:
                    pe.wait_ge(cT_ready.sem, cT_ready.at(i, m + 1))
                else:
                    pe.wait_ge(h_ready.sem, h_ready.at(i, TE * m + n - 1))
                pe.matmul(flat(C), w["pairs"][:, n - 1], flat(cT[m % 2]), start=True,
                          stop=True).then_inc(weight_ready.sem, 1)

            def side_transposes(i, k):
                pe.wait_ge(side_done.sem, side_done.at(i, k))
                pe.wait_ge(sz_ready.sem, sz_ready.at(i, k + 1))
                for t in range(T):
                    mm = pe.transpose(S[0][:, t], zs[:, t], w["ident"][:])
                mm.then_inc(szT_ready.sem, 1)

            def side_input(i, k):
                pe.wait_ge(xls_ready.sem, xls_ready.at(i, k + 1))

            def hidden(m, k, i):
                if k > 0:
                    pe.wait_ge(hid_ready.sem, hid_ready.at(i, FT * nth(m) + k))
                product(S[1], w["w1h"][:, k], w["w1l"][:, k], xhs, xls).then_inc(hid_mm.sem, 1)

            def mlp_down(m, k, i):
                pe.wait_ge(hid_ready.sem, hid_ready.at(i, FT * nth(m) + k + 1))
                mm = down(S[0], hs[k % 2], w["w2"][:, k], k == 0)
                if k == FT - 1:
                    mm.then_inc(side_mm.sem, 1)

            def kvu_product(m, ts, i):
                a = nth(m)
                for t in ts:
                    if t >= 2:
                        pe.wait_ge(kvu_out.sem, kvu_out.at(i, T * a + t - 1))
                    o = flat(S[1 - t % 2])[:, 0:3 * D]
                    pe.matmul(o, xhs[:, t], w["wkvuh"][:], start=True, stop=False)
                    pe.matmul(o, xhs[:, t], w["wkvul"][:], start=False, stop=False)
                    pe.matmul(o, xls[:, t], w["wkvuh"][:], start=False, stop=True).then_inc(kvu_mm.sem, 1)

            def queries(a, i):
                pe.wait_ge(kvu_out.sem, kvu_out.at(i, T * a + 3))
                product(S[1], w["wqh"][:], w["wql"][:], xhs, xls).then_inc(q_mm.sem, 1)

            def keys_values(a, i):
                pe.wait_ge(kc_ready.sem, kc_ready.at(i, a + 1))
                pe.wait_ge(ks_ready.sem, ks_ready.at(i, a + 1))
                for c in range(2):
                    for t in range(T):
                        mm = pe.matmul(S[0][:, c], kc[:, c, t], kvu[:, t, D:2 * D], start=(t == 0),
                                       stop=(t == T - 1), skip_group_check=True)
                mm.then_inc(kv_mm.sem, 1)

            def attend(a, i):
                pe.wait_ge(qc_ready.sem, qc_ready.at(i, a + 1))
                pe.wait_ge(kvm_ready.sem, kvm_ready.at(i, a + 1))
                for t in range(T):
                    for c in range(2):
                        mm = pe.matmul(S[1][:, t], qc[:, c, t], kvm[:, c], start=(c == 0), stop=(c == 1),
                                       skip_group_check=True)
                mm.then_inc(o_mm.sem, 1)

            def out_transposes(a, i):
                pe.wait_ge(og_ready.sem, og_ready.at(i, a + 1))
                for t in range(T):
                    mm = pe.transpose(S[0][:, t], og[:, t], w["ident"][:])
                mm.then_inc(oT_mm.sem, 1)

            def slot(m, i, side, prepare):
                g0, a, steps = NT * m, nth(m), PREPARE[side or MLP]
                high, low = xh[m % 2], xl[m % 2]
                pe.wait_ge(xl_ready.sem, xl_ready.at(i, m + 1))
                for n in range(NT):
                    if n >= 2:
                        pe.wait_ge(act_done.sem, act_done.at(i, g0 + n - 1))
                    product(G[n % 2], w["wgh"][:, n], w["wgl"][:, n], high, low).then_inc(gate_ready.sem, 1)
                    if n >= 1:
                        pe.wait_ge(up_used.sem, up_used.at(i, g0 + n))
                    product(U, w["wuh"][:, n], w["wul"][:, n], high, low).then_inc(up_ready.sem, 1)
                    if n == 0:
                        comb_transposes(m, i)
                    else:
                        routing_weights(m, n, i)
                    if n == 2 and side:
                        side_input(i, m)
                    if side == ATT:
                        if n == 2:
                            kvu_product(m, (0, 1), i)
                        if n == 3:
                            kvu_product(m, (2, 3), i)
                        if n == 5:
                            attend(a, i)
                        if n == 8:
                            out_transposes(a, i)
                    if side == MLP:
                        if 2 <= n < 2 + FT:
                            hidden(m, n - 2, i)
                        if 3 <= n < 3 + FT:
                            mlp_down(m, n - 3, i)
                    if prepare and n == steps["transpose"]:
                        main_transposes(m + 1, i)
                    if prepare and n == steps["logits"]:
                        logits(m + 1, i)
                    if n >= 1:
                        moe_down(m, n - 1, i)
                    if n == 1 and side:
                        side_transposes(i, m)
                    if side == ATT:
                        if n == 3:
                            queries(a, i)
                        if n == 4:
                            keys_values(a, i)
                        if n == 8:
                            pe.wait_ge(oT_ready.sem, oT_ready.at(i, a + 1))
                            down(S[1], oT, w["wout"][:], True).then_inc(side_mm.sem, 1)
                moe_down(m, NT - 1, i)

            main_transposes(-1, 0)
            logits(-1, 0)
            slot(-1, 0, None, True)
            with pe.Fori(0, turns) as i:
                for m in range(NM):
                    slot(m, i, SIDE[m], True)
            slot(0, turns, None, False)
            side_transposes(turns, 0)
            side_input(turns, 0)
            for k in range(FT):
                hidden(1, k, turns)
                mlp_down(1, k, turns)


SCHEDULE = [
    [("qk", 0, 4)], [("ot", -1, 3), ("qk", 0, 5)], [], [("nm", 0, 1), ("qk", 0, 6)],
    [], [("ot", 0, 0), ("qk", 0, 7)], [], [("nm", 0, 2), ("xt", 1, 0)],
    [("qk", 1, 0), ("ft", -1, 0)], [("ot", 0, 1), ("qk", 1, 1)], [("g", -1, 0), ("v", 1, 0)],
    [("nm", 0, 3), ("g", -1, 1)], [("g", -1, 2), ("qk", 1, 2), ("g", -1, 3)], [("ot", 0, 2), ("qk", 1, 3)],
    [], [("y", -1, 0), ("nm", 1, 0)]]
SMALL = sum(SCHEDULE, [])
STEPS = GRP * T
AHEAD = 5
UNITS = STEPS * HG
ST_BANKS, MX_BANKS = 2, 3
BACK_DVE = 2 * (3 + GRP)
BACK_POOL = 2 * 7


def build_back(nc, weights, mid_dram, out_dram, batches):
    w = weights
    with ExitStack() as ctx:
        def sb(name, shape, dt=F32):
            return ctx.enter_context(nc.sbuf_tensor("b_" + name, shape, dt))

        def ps(name, shape=(P, T, P)):
            return ctx.enter_context(nc.psum_tensor("b_" + name, list(shape), F32))

        def sig(name, per):
            return Signal(ctx.enter_context(nc.semaphore("b_" + name)), per)

        x = [sb(f"x{p}", [P, T, D]) for p in range(2)]
        z = sb("z", [P, T, D])
        xn = sb("xn", [P, T, D])
        xx = [sb(f"xx{p}", [P, T, D]) for p in range(2)]
        xh = [sb(f"xh{p}", [P, T, P], F32R) for p in range(2)]
        xl = [sb(f"xl{p}", [P, T, P], F32R) for p in range(2)]
        part = [sb(f"part{k}", [P, T, P], F32R) for k in range(2)]
        qt = [sb(f"qt{g}", [P, T, P], F32R) for g in range(GRP)]
        kt_ = [sb(f"kt{g}", [P, T, P], F32R) for g in range(GRP)]
        kz = [sb(f"kz{g}", [P, HG, T, P], F32R) for g in range(GRP)]
        qm = [sb(f"qm{k}", [P, T, P], F32R) for k in range(2)]
        nm = [sb(f"nm{k}", [P, T, P]) for k in range(2)]
        va = [sb(f"va{p}", [P, T, H, 32]) for p in range(2)]
        pr = [sb(f"pr{k}", [P, HG, N]) for k in range(2)]
        oTs = [sb(f"oTs{k}", [P, T, P]) for k in range(2)]
        rden = sb("rden", [P, T, HG, 1])
        osum = sb("osum", [P, T, D])
        xf = sb("xf", [P, T, D])
        xfb = sb("xfb", [P, T, D])
        zf = sb("zf", [P, T, D])
        fh = sb("fh", [P, T, P], F32R)
        fl = sb("fl", [P, T, P], F32R)
        hid = [sb(f"hid{n}", [P, T, P]) for n in range(FT)]
        res = [sb(f"res{p}", [P, T, D]) for p in range(2)]
        nudge = sb("nudge", [P, 1])
        norm = {k: (sb(f"st{k}", [P, T, 6]), sb(f"mv{k}", [P, T, 2]), sb(f"ve{k}", [P, T]), sb(f"rs{k}", [P, T, 1]))
                for k in ("1", "2", "f")}

        ST = [ps(f"ST{k}") for k in range(ST_BANKS)]
        MX = [ps(f"MX{k}") for k in range(MX_BANKS)]
        PV = ps("PV")
        M = [ps(f"M{k}") for k in range(2)]

        loaded = [sig(f"loaded{p}", 16) for p in range(2)]
        stored = [sig(f"stored{p}", 16) for p in range(2)]
        mv_ready = {k: sig(f"mv_ready{k}", 1) for k in norm}
        rs_ready = {k: sig(f"rs_ready{k}", 1) for k in norm}
        z1_ready = sig("z1_ready", 1)
        zf_ready = sig("zf_ready", 1)
        xn_ready = sig("xn_ready", 1)
        xx_ready = sig("xx_ready", 1)
        xfb_ready = sig("xfb_ready", 1)
        xf_ready = sig("xf_ready", 1)
        xh_ready = sig("xh_ready", 1)
        fh_ready = sig("fh_ready", 1)
        part_ready = sig("part_ready", 2 * GRP)
        spread = [sig(f"spread{g}", 16 * HG) for g in range(GRP)]
        cleared = ctx.enter_context(nc.semaphore("b_cleared"))
        scores_mm = sig("scores_mm", UNITS)
        exp_done = sig("exp_done", UNITS)
        pv_mm = sig("pv_mm", STEPS)
        pv_out = sig("pv_out", GRP)
        first_mm = sig("first_mm", UNITS)
        max_done = sig("max_done", UNITS)
        per = {"qk": 2 * GRP, "ot": GRP, "nm": GRP, "ft": 1, "g": FT, "y": 1, "xt": 1, "v": 1}
        made = {k: sig(f"made_{k}", n) for k, n in per.items()}
        used = {k: sig(f"used_{k}", n) for k, n in per.items()}
        dve_own = ctx.enter_context(nc.semaphore("b_dve_own"))
        pool_own = ctx.enter_context(nc.semaphore("b_pool_own"))

        md = mid_dram.rearrange("b (p t) d -> b p t d", p=P)
        od = out_dram.rearrange("b (p t) d -> b p t d", p=P)

        class Batch:

            def __init__(self, turn, off):
                self.turn, self.off = turn, off
                self.parity = off % 2
                known = isinstance(turn, int)
                self.exists = not known or 0 <= 2 * turn + off < batches

            def __add__(self, k):
                return Batch(self.turn, self.off + k)

            @property
            def number(self):
                return self.turn * 2 + self.off

            def at(self, signal, n):
                return self.turn * (2 * signal.per) + (self.off * signal.per + n)

            def at_own(self, signal, n):
                return self.turn * signal.per + ((self.off - self.parity) // 2 * signal.per + n)

        def bank_of(name, n):
            return M[[(a, c) for a, _, c in SMALL].index((name, n)) % 2]

        def program(eng, batch_steps, chain=None):
            for off in (-1, 0, 1):
                batch_steps(Batch(0, off))
            last = batches // 2 - 1
            if last > 1:
                with eng.Fori(1, last) as i:
                    if chain:
                        chain.enter(i - 1)
                    batch_steps(Batch(i, 0))
                    batch_steps(Batch(i, 1))
                    if chain:
                        chain.leave(last - 1)
            for off in (0, 1, 2):
                batch_steps(Batch(last, off))

        block = ctx.enter_context(nc.Block())

        @block.sync
        def _(sp):
            def spread_keys(B, g):
                if not B.exists:
                    return
                if isinstance(B.turn, int) and B.number == 0:
                    sp.wait_ge(cleared, g + 1)
                sp.wait_ge(used["qk"].sem, B.at(used["qk"], 2 * g + 1))
                for j in range(HG):
                    rows = slice(32 * j, 32 * j + 32)
                    sp.dma_start(kz[g][rows, j].bitcast(F32), kt_[g][rows].bitcast(F32)).then_inc(spread[g].sem, 16)

            def batch_steps(B):
                nxt, prv = B + 1, B + -1
                ahead = B + 2
                if ahead.exists:
                    if B.exists:
                        sp.wait_ge(xx_ready.sem, B.at(xx_ready, 1))
                    p = ahead.parity
                    sp.dma_start(x[p][:], md[ahead.number + PAD]).then_inc(loaded[p].sem, 16)
                spread_keys(B, 2)
                spread_keys(B, 3)
                spread_keys(nxt, 0)
                spread_keys(nxt, 1)
                if prv.exists:
                    p = prv.parity
                    sp.wait_ge(used["y"].sem, prv.at(used["y"], 1))
                    sp.dma_start(od[prv.number], res[p][:]).then_inc(stored[p].sem, 16)

            sp.dma_start(x[0][:], md[PAD]).then_inc(loaded[0].sem, 16)
            program(sp, batch_steps)
            for p in range(2):
                sp.wait_ge(stored[p].sem, 16 * (batches // 2))

        @block.gpsimd
        def _(pool):
            own = Chain(pool, pool_own, BACK_POOL)

            def rsqrt(k, B, eps):
                _, mv, ve, rs = norm[k]
                pool.wait_ge(mv_ready[k].sem, B.at(mv_ready[k], 1))
                own.step(nc.gpsimd.tensor_tensor(ve[:], mv[:, :, 1], w[eps][:], ALU.add))
                own.settle()
                nc.gpsimd.tensor_tensor(rs[:, :, 0], ve[:], w["minus_half"][:], ALU.pow).then_inc(rs_ready[k].sem, 1)

            def normalise(k, src, B):
                _, mv, _, rs = norm[k]
                pool.wait_ge(rs_ready[k].sem, B.at(rs_ready[k], 1))
                own.step(nc.gpsimd.tensor_tensor(z[:], src[:], mv[:, :, 0:1].broadcast_to([P, T, D]), ALU.subtract))
                own.settle()
                return nc.gpsimd.tensor_tensor(z[:], z[:], rs[:].broadcast_to([P, T, D]), ALU.mult)

            def batch_steps(B):
                nxt, prv = B + 1, B + -1
                if nxt.exists:
                    rsqrt("1", nxt, "eps")
                    normalise("1", x[nxt.parity], nxt).then_inc(z1_ready.sem, 1)
                if prv.exists:
                    pool.wait_ge(used["ot"].sem, prv.at(used["ot"], GRP))
                    if not isinstance(prv.turn, int) or prv.number >= 1:
                        pool.wait_ge(xfb_ready.sem, prv.at(xfb_ready, 0))
                        pool.wait_ge(zf_ready.sem, prv.at(zf_ready, 0))
                    nc.gpsimd.tensor_tensor(xf[:], osum[:], xx[prv.parity][:], ALU.add).then_inc(xf_ready.sem, 1)
                    rsqrt("f", prv, "eps")
                if nxt.exists:
                    rsqrt("2", nxt, "eps_in")
                    own.step(normalise("2", z, nxt))
                    own.settle()
                    own.step(nc.gpsimd.tensor_tensor(xn[:], z[:], w["lns"][:], ALU.mult))
                    own.settle()
                    nc.gpsimd.tensor_tensor(xn[:], xn[:], w["lnsb"][:], ALU.add).then_inc(xn_ready.sem, 1)
                    pool.wait_ge(xn_ready.sem, nxt.at(xn_ready, 1))
                    nc.gpsimd.tensor_tensor(xx[nxt.parity][:], x[nxt.parity][:], xn[:],
                                            ALU.add).then_inc(xx_ready.sem, 1)
                if prv.exists:
                    pool.wait_ge(xf_ready.sem, prv.at(xf_ready, 1))
                    nc.gpsimd.tensor_tensor(xfb[:], xf[:], w["b2h"][:], ALU.add).then_inc(xfb_ready.sem, 1)

            for p in range(2):
                own.step(nc.gpsimd.memset(va[p][:], 0.0))
                own.settle()
                own.step(nc.gpsimd.memset(va[p][:, :, :, DH:DH + 1], 1.0))
            own.settle()
            program(pool, batch_steps, own)

        @block.scalar
        def _(act):
            def small(B, name, n):
                if not B.exists:
                    return
                p = B.parity
                act.wait_ge(made[name].sem, B.at(made[name], n + 1))
                m = bank_of(name, n)
                if name == "qk":
                    if not isinstance(B.turn, int) or B.number * 2 * GRP + n >= 2:
                        act.wait_ge(used["qk"].sem, B.at(used["qk"], n - 1))
                    if n % 2 == 1:
                        ins = nc.scalar.activation(part[0][:], m[:], ACT.Copy, scale=w["keep"][:, 0:1])
                    else:
                        ins = nc.scalar.activation(part[1][:], m[:], ACT.Identity, scale=w["keep"][:, 2:3],
                                                   bias=w["keep"][:, 4:5])
                    ins.then_inc(part_ready.sem, 1)
                elif name == "xt":
                    nc.scalar.activation(xh[p][:], m[:], ACT.Copy).then_inc(xh_ready.sem, 1)
                elif name == "ft":
                    nc.scalar.activation(fh[:], m[:], ACT.Copy).then_inc(fh_ready.sem, 1)
                elif name == "v":
                    nc.scalar.activation(va[p][:, :, :, 0:DH], m[:].rearrange("p t (h e) -> p t h e", h=H),
                                         ACT.Copy).then_inc(used["v"].sem, 1)
                elif name == "g":
                    nc.scalar.activation(hid[n][:], m[:], ACT.Relu, bias=w["b1"][:, n:n + 1]).then_inc(used["g"].sem, 1)

            def weights_out(B, g):
                if B.exists:
                    act.wait_ge(pv_mm.sem, B.at(pv_mm, T * (g + 1)))
                    nc.scalar.activation(oTs[g % 2][:], PV[:], ACT.Copy).then_inc(pv_out.sem, 1)

            def batch_steps(B):
                nxt, prv = B + 1, B + -1
                for k in range(STEPS):
                    for j in range(HG):
                        if B.exists:
                            u = k * HG + j
                            act.wait_ge(scores_mm.sem, B.at(scores_mm, u + 1))
                            if j == 0 and (k >= 2 or not isinstance(B.turn, int) or B.number > 0):
                                act.wait_ge(pv_mm.sem, B.at(pv_mm, k - 1))
                            nc.scalar.activation(pr[k % 2][:, j], ST[u % ST_BANKS][:].rearrange("p a b -> p (a b)"),
                                                 ACT.Exp, scale=SM_SCALE).then_inc(exp_done.sem, 1)
                        if j == 1 and k % T == 0:
                            if k == 0:
                                weights_out(prv, GRP - 1)
                            else:
                                weights_out(B, k // T - 1)
                        if j >= 2:
                            for name, rel, n in SCHEDULE[k][:1] if j == 2 else SCHEDULE[k][1:]:
                                if name not in ("ot", "nm", "y"):
                                    small(B + rel, name, n)

            for g in range(GRP):
                nc.scalar.activation(kz[g][:].rearrange("p j t c -> p (j t) c"),
                                     w["ident"][:].rearrange("p (o c) -> p o c", o=1).broadcast_to([P, HG * T, P]),
                                     ACT.Copy, scale=0.0).then_inc(cleared, 1)
            program(act, batch_steps)

        @block.vector
        def _(dve):
            own = Chain(dve, dve_own, BACK_DVE)

            def stats(k, src):
                st, mv, _, _ = norm[k]
                for t in range(T):
                    ins = nc.vector.bn_stats(st[:, t], src[:, t])
                own.step(ins)
                own.settle()
                nc.vector.memset(nudge[:], 0.0)
                for t in range(T):
                    ins = nc.vector.bn_aggr(mv[:, t], st[:, t])
                ins.then_inc(mv_ready[k].sem, 1)

            def normalise(k, out, src, B, done):
                _, mv, _, rs = norm[k]
                dve.wait_ge(rs_ready[k].sem, B.at(rs_ready[k], 1))
                for t in range(T):
                    ins = nc.vector.tensor_scalar(out[:, t], src[:, t], mv[:, t, 0:1], rs[:, t],
                                                  ALU.subtract, ALU.mult)
                ins.then_inc(done.sem, 1)

            def small(B, name, n):
                if not B.exists:
                    return
                p = B.parity
                m = bank_of(name, n)
                if name == "qk":
                    dve.wait_ge(part_ready.sem, B.at(part_ready, n + 1))
                    out, c = (kt_ if n % 2 == 0 else qt)[n // 2], 3 if n % 2 == 0 else 1
                    if n % 2 == 0 and (not isinstance(B.turn, int) or B.number > 0):
                        dve.wait_ge(spread[n // 2].sem, B.at(spread[n // 2], 0))
                    nc.vector.scalar_tensor_tensor(out=out[:], in0=m[:], scalar=w["keep"][:, c:c + 1],
                                                   in1=part[1 - n % 2][:], op0=ALU.mult,
                                                   op1=ALU.add).then_inc(used["qk"].sem, 1)
                elif name == "xt":
                    dve.wait_ge(xh_ready.sem, B.at(xh_ready, 1))
                    nc.vector.tensor_tensor(xl[p][:], m[:], xh[p][:], ALU.subtract).then_inc(used["xt"].sem, 1)
                elif name == "ft":
                    dve.wait_ge(fh_ready.sem, B.at(fh_ready, 1))
                    nc.vector.tensor_tensor(fl[:], m[:], fh[:], ALU.subtract).then_inc(used["ft"].sem, 1)
                elif name == "nm":
                    dve.wait_ge(made["nm"].sem, B.at(made["nm"], n + 1))
                    nc.vector.tensor_tensor(qm[n % 2][:], qt[n][:], m[:], ALU.subtract).then_inc(used["nm"].sem, 1)
                elif name == "ot":
                    dve.wait_ge(made["ot"].sem, B.at(made["ot"], n + 1))
                    if n > 0 or not isinstance(B.turn, int) or B.number > 0:
                        dve.wait_ge(used["ot"].sem, B.at(used["ot"], n))
                    o = m[:].rearrange("p t (j r) -> p t j r", j=HG)
                    if n == 0 and (not isinstance(B.turn, int) or B.number > 0):
                        dve.wait_ge(xf_ready.sem, B.at(xf_ready, 0))
                    own.step(nc.vector.reciprocal(rden[:], o[:, :, :, DH:DH + 1]))
                    own.settle()
                    for t in range(T):
                        ins = nc.vector.tensor_tensor(
                            osum[:, t, n * HG * DH:(n + 1) * HG * DH].rearrange("p (j e) -> p j e", j=HG),
                            o[:, t, :, 0:DH], rden[:, t].broadcast_to([P, HG, DH]), ALU.mult)
                    ins.then_inc(used["ot"].sem, 1)
                elif name == "y":
                    dve.wait_ge(made["y"].sem, B.at(made["y"], 1))
                    dve.wait_ge(xfb_ready.sem, B.at(xfb_ready, 1))
                    if not isinstance(B.turn, int) or B.number >= 2:
                        dve.wait_ge(stored[p].sem, B.at_own(stored[p], 0))
                    nc.vector.scalar_tensor_tensor(out=res[p][:], in0=m[:], scalar=0.5, in1=xfb[:], op0=ALU.mult,
                                                   op1=ALU.add).then_inc(used["y"].sem, 1)

            def side(B, k):
                nxt, prv = B + 1, B + -1
                if k == 0 and nxt.exists:
                    p = nxt.parity
                    dve.wait_ge(loaded[p].sem, nxt.at_own(loaded[p], 16))
                    stats("1", x[p])
                if k == 2 and prv.exists:
                    dve.wait_ge(xf_ready.sem, prv.at(xf_ready, 1))
                    stats("f", xf)
                if k == 4 and nxt.exists:
                    dve.wait_ge(z1_ready.sem, nxt.at(z1_ready, 1))
                    stats("2", z)
                if k == 6 and prv.exists:
                    normalise("f", zf, xf, prv, zf_ready)

            def maximum(B, u):
                g, j, t = u // (HG * T), u // T % HG, u % T
                dve.wait_ge(first_mm.sem, B.at(first_mm, u + 1))
                c = 32 * j + MAX_ROW
                nc.vector.tensor_reduce(nm[g % 2][:, t, c:c + 1], MX[u % MX_BANKS][:].rearrange("p a b -> p (a b)"), AX.X,
                                        ALU.max).then_inc(max_done.sem, 1)

            def batch_steps(B):
                for k in range(STEPS):
                    C, s = (B, k + AHEAD) if k + AHEAD < STEPS else (B + 1, k + AHEAD - STEPS)
                    if C.exists:
                        for t in range(2):
                            maximum(C, s * T + t)
                    for name, rel, n in SCHEDULE[k]:
                        if name == "nm":
                            small(B + rel, name, n)
                    if C.exists:
                        for t in range(2, T):
                            maximum(C, s * T + t)
                    for name, rel, n in SCHEDULE[k]:
                        if name not in ("v", "g", "nm"):
                            small(B + rel, name, n)
                    side(B, k)

            for k in range(2):
                own.step(nc.vector.memset(nm[k][:], 0.0))
            own.settle()
            program(dve, batch_steps, own)

        @block.tensor
        def _(pe):
            def flat(t):
                return t[:].rearrange("p a b -> p (a b)")

            def product(bank, wh, wl, a, b):
                pe.matmul(flat(bank), wh, flat(a), start=True, stop=False)
                pe.matmul(flat(bank), wl, flat(a), start=False, stop=False)
                return pe.matmul(flat(bank), wh, flat(b), start=False, stop=True)

            def wait_small_bank(B, pos):
                here = B + -SMALL[pos][1]
                for back in range(2, len(SMALL), 2):
                    before_name, before_rel, before_n = SMALL[pos - back]
                    other = here + (before_rel - (1 if pos < back else 0))
                    if other.exists:
                        pe.wait_ge(used[before_name].sem, other.at(used[before_name], before_n + 1))
                        break

            def mlp_out(B, t):
                if not B.exists:
                    return
                m = bank_of("y", 0)
                if t == 0:
                    wait_small_bank(B, SMALL.index(("y", -1, 0)))
                    pe.wait_ge(used["g"].sem, B.at(used["g"], FT))
                for f in range(FT):
                    mm = pe.matmul(m[:, t], hid[f][:, t], w["w2"][:, f], start=(f == 0), stop=(f == FT - 1),
                                   skip_group_check=True)
                if t == T - 1:
                    mm.then_inc(made["y"].sem, 1)

            def small(B, name, n):
                if not B.exists:
                    return
                p = B.parity
                pos = [(a, c) for a, _, c in SMALL].index((name, n))
                m = M[pos % 2]
                wait_small_bank(B, pos)
                if name == "qk":
                    g = n // 2
                    pe.wait_ge(used["xt"].sem, B.at(used["xt"], 1))
                    r = "kr" if n % 2 == 0 else "qr"
                    mm = product(m, w[r + "h"][:, g], w[r + "l"][:, g], xh[p], xl[p])
                elif name == "xt":
                    pe.wait_ge(xn_ready.sem, B.at(xn_ready, 1))
                    for t in range(T):
                        mm = pe.transpose(m[:, t], xn[:, t], w["ident"][:])
                elif name == "ft":
                    pe.wait_ge(zf_ready.sem, B.at(zf_ready, 1))
                    for t in range(T):
                        mm = pe.transpose(m[:, t], zf[:, t], w["ident"][:])
                elif name == "v":
                    pe.wait_ge(used["xt"].sem, B.at(used["xt"], 1))
                    for t in range(T):
                        pe.matmul(m[:, t], xh[p][:, t], w["wvh"][:], start=True, stop=False, skip_group_check=True)
                        pe.matmul(m[:, t], xh[p][:, t], w["wvl"][:], start=False, stop=False, skip_group_check=True)
                        mm = pe.matmul(m[:, t], xl[p][:, t], w["wvh"][:], start=False, stop=True,
                                       skip_group_check=True)
                elif name == "nm":
                    pe.wait_ge(max_done.sem, B.at(max_done, (n + 1) * HG * T))
                    for t in range(T):
                        mm = pe.transpose(m[:, t], nm[n % 2][:, t], w["ident"][:])
                elif name == "ot":
                    pe.wait_ge(pv_out.sem, B.at(pv_out, n + 1))
                    for t in range(T):
                        mm = pe.transpose(m[:, t], oTs[n % 2][:, t], w["ident"][:])
                else:
                    pe.wait_ge(used["ft"].sem, B.at(used["ft"], 1))
                    mm = product(m, w["w1h"][:, n], w["w1l"][:, n], fh, fl)
                mm.then_inc(made[name].sem, 1)

            def wait_bank(B, u, done, banks):
                if u >= banks:
                    pe.wait_ge(done.sem, B.at(done, u - banks + 1))
                elif not isinstance(B.turn, int) or B.number > 0:
                    last = max(v for v in range(UNITS) if v % banks == u % banks)
                    pe.wait_ge(done.sem, B.at(done, last + 1 - UNITS))

            def scores(B, k, j):
                g, u = k // T, k * HG + j
                if k % T == 0 and j == 0:
                    pe.wait_ge(used["nm"].sem, B.at(used["nm"], g + 1))
                wait_bank(B, u, exp_done, ST_BANKS)
                pe.matmul(flat(ST[u % ST_BANKS]), kz[g][:, j, k % T], flat(qm[g % 2]), start=True,
                          stop=True).then_inc(scores_mm.sem, 1)

            def first_scores(B, s, t):
                u = s * T + t
                g, j = u // (HG * T), u // T % HG
                if t == 0 and j == 0:
                    pe.wait_ge(spread[g].sem, B.at(spread[g], 16 * HG))
                    pe.wait_ge(used["qk"].sem, B.at(used["qk"], 2 * g + 2))
                wait_bank(B, u, max_done, MX_BANKS)
                pe.matmul(flat(MX[u % MX_BANKS]), qt[g][:, t], kz[g][:, j].rearrange("p a b -> p (a b)"), start=True,
                          stop=True).then_inc(first_mm.sem, 1)

            def weighted(B, k):
                if not B.exists:
                    return
                g, kt = k // T, k % T
                pe.wait_ge(exp_done.sem, B.at(exp_done, HG * (k + 1)))
                if kt == 0:
                    if g == 0:
                        pe.wait_ge(used["v"].sem, B.at(used["v"], 1))
                    if g > 0 or not isinstance(B.turn, int) or B.number > 0:
                        pe.wait_ge(pv_out.sem, B.at(pv_out, g))
                for j in range(HG):
                    mm = pe.matmul(flat(PV)[32 * j:32 * j + 32], va[B.parity][:, kt, g * HG + j], pr[k % 2][:, j],
                                   start=(kt == 0), stop=(kt == T - 1), skip_group_check=True)
                mm.then_inc(pv_mm.sem, 1)

            def batch_steps(B):
                for k in range(STEPS):
                    C, s = (B, k + AHEAD) if k + AHEAD < STEPS else (B + 1, k + AHEAD - STEPS)
                    for j in range(HG):
                        if B.exists:
                            scores(B, k, j)
                        if C.exists:
                            first_scores(C, s, j)
                        if j == 0:
                            if k == 0:
                                weighted(B + -1, STEPS - 1)
                            else:
                                weighted(B, k - 1)
                        if k >= STEPS - 2 and j % 2 == 1:
                            mlp_out(B + -1, (k - (STEPS - 2)) * 2 + j // 2)
                        others = [one for one in SCHEDULE[k] if one[0] != "y"]
                        if j >= 2:
                            for name, rel, n in others[:1] if j == 2 else others[1:]:
                                small(B + rel, name, n)

            program(pe, batch_steps)


BACK_WEIGHTS = ("ident", "b1", "b2h", "w2", "lns", "lnsb", "keep", "w1h", "w1l", "qrh", "qrl", "krh", "krl", "wvh",
                "wvl", "minus_half", "eps", "eps_in")


def build_weights(nc, front, back, a):
    w, wanted = {}, {}

    def sb(name, shape, dt=F32):
        wanted[name] = (shape, dt)

    plain = {
        "ident": ([P, P], a["c_ident"]),
        "ramp": ([P, T, E], a["c_ramp"]),
        "heads": ([P, 2, D], a["c_heads"]),
        "wout": ([P, D], a["wout_t"]),
        "bq": ([P, 1], a["bq"]),
        "bkvu": ([P, 3 * D], a["bkvu"]),
        "bout": ([P, T, D], a["bout"]),
        "lnw": ([P, T, D], a["lnw"]),
        "lnb": ([P, T, D], a["lnb"]),
        "b1": ([P, FT], a["b1"]),
        "b2h": ([P, T, D], a["b2"]),
        "w2": ([P, FT, D], a["w2"].rearrange("(n p) d -> p n d", p=P)),
        "lns": ([P, T, D], a["lns"]),
        "lnsb": ([P, T, D], a["lnsb"]),
        "keep": ([P, 5], a["c_keep"]),
    }
    for name, (shape, _) in plain.items():
        sb(name, shape)
    sb("wd", [P, NT, D])
    for name in ("minus_half", "eps", "eps_in"):
        sb(name, [P, T])
    parts = {
        "router": (None, None),
        "wg": [P, NT, P], "wu": [P, NT, P], "wq": [P, P], "wkvu": [P, 3 * D], "w1": [P, FT, P],
        "qr": [P, GRP, P], "kr": [P, GRP, P], "wv": [P, D],
    }
    sb("router", [P, 2 * E], F32R)
    sb("pairs", [2 * E, TE, P], F32R)
    for name, shape in parts.items():
        if name != "router":
            sb(name + "h", shape, F32R)
            sb(name + "l", shape, F32R)
    for name in ("cos_t", "sin_t", "cos_c", "sin_c"):
        sb(name, [P, T, P])
    for scope, keep in ((back, True), (front, False)):
        for name, (shape, dt) in wanted.items():
            if (name in BACK_WEIGHTS) == keep:
                w[name] = scope.enter_context(nc.sbuf_tensor("w_" + name, shape, dt))

    with ExitStack() as tmp:
        def scratch(name, shape, dt=F32):
            return tmp.enter_context(nc.sbuf_tensor("t_" + name, shape, dt))

        raw = {name: scratch(name, shape) for name, shape in parts.items() if name != "router"}
        router = scratch("router", [P, E])
        pairs = scratch("pairs", [2 * E, TE, P])
        theta_t = scratch("theta_t", [P, T, P])
        pos_t = scratch("pos_t", [P, T, P])
        turns_ = scratch("turns", [P, T, P])
        angle = {f: scratch("angle_" + f, [P, T, P]) for f in ("sin", "cos")}
        turned = {f: tmp.enter_context(nc.psum_tensor("t_turned_" + f, [P, T, P], F32)) for f in angle}

        def sem(name):
            return tmp.enter_context(nc.semaphore("w_" + name))

        group = {
            "tables": [(theta_t[:], a["theta_t"]), (pos_t[:], a["c_pos_t"]), (w["ident"][:], plain["ident"][1])],
            "moe": [(router[:], a["gate_t"]),
                    (raw["wg"][:, 0], a["Ws_gate"]), (raw["wg"][:, 1:], a["we_gate_t"]),
                    (raw["wu"][:, 0], a["Ws_up"]), (raw["wu"][:, 1:], a["we_up_t"])],
            "others": [(pairs[:], a["c_pairs"]),
                       (raw["wq"][:], a["wqkvu_t"][:, 0:D]), (raw["wkvu"][:], a["wqkvu_t"][:, D:]),
                       (raw["w1"][:], a["w1"].rearrange("h (n w) -> h n w", n=FT)),
                       (raw["qr"][:], a["q_rep"].rearrange("h (g c) -> h g c", g=GRP)),
                       (raw["kr"][:], a["k_rep"].rearrange("h (g c) -> h g c", g=GRP)),
                       (raw["wv"][:], a["wv"])],
            "down": [(w["wd"][:, 0], a["Ws_down"]),
                     (w["wd"][:, 1:], a["We_down"].rearrange("(n e) i h -> (e i) n h", e=2))],
            "plain": [(w[n][:], src) for n, (_, src) in plain.items() if n != "ident"],
        }
        loaded = {g: sem("loaded_" + g) for g in group}
        high_ready, angle_ready, table_ready, turned_ready = (
            sem(n) for n in ("high_ready", "angle_ready", "table_ready", "turned_ready"))
        dve_own = sem("dve")
        block = tmp.enter_context(nc.Block())

        def load(eng, g):
            for dst, src in group[g]:
                eng.dma_start(dst, src).then_inc(loaded[g], 16)

        def wait_loads(eng, g):
            eng.wait_ge(loaded[g], 16 * len(group[g]))

        halves = [(router[:], w["router"][:, 0:E], w["router"][:, E:2 * E])]
        halves += [(raw[n][:], w[n + "h"][:], w[n + "l"][:]) for n in raw]
        first_others = 1 + list(raw).index("wq")
        first_dve = 1 + list(raw).index("qr")

        def low_parts(eng, ops, which):
            for k in which:
                whole, high, low = halves[k]
                eng.wait_ge(high_ready, k + 1)
                ops.tensor_tensor(low, whole, high, ALU.subtract)

        @block.sync
        def _(sp):
            for g in ("tables", "others", "plain"):
                load(sp, g)
            for g in ("down", "plain"):
                wait_loads(sp, g)

        @block.gpsimd
        def _(pool):
            nc.gpsimd.memset(w["minus_half"][:], -0.5)
            nc.gpsimd.memset(w["eps"][:], EPS)
            nc.gpsimd.memset(w["eps_in"][:], EPS_IN)
            low_parts(pool, nc.gpsimd, range(first_dve))

        @block.vector
        def _(dve):
            own = Chain(dve, dve_own, 0)
            wait_loads(dve, "tables")
            theta = theta_t
            own.step(nc.vector.tensor_tensor(theta[:], theta[:], pos_t[:], ALU.mult))
            for f, quarter in (("sin", 0.0), ("cos", 0.25)):
                own.settle()
                own.step(nc.vector.tensor_scalar(turns_[:], theta[:], float(1 / (2 * np.pi)), quarter,
                                                 ALU.mult, ALU.add))
                own.settle()
                own.step(nc.vector.tensor_scalar(turns_[:], turns_[:], BIG_ROUND, None, ALU.add))
                own.settle()
                own.step(nc.vector.tensor_scalar(turns_[:], turns_[:], -BIG_ROUND, None, ALU.add))
                r = angle[f]
                src = theta
                for part in TWO_PI:
                    own.settle()
                    own.step(nc.vector.scalar_tensor_tensor(out=r[:], in0=turns_[:], scalar=-part, in1=src[:],
                                                            op0=ALU.mult, op1=ALU.add))
                    src = r
                own.settle()
                own.step(nc.vector.tensor_scalar(r[:], r[:], float(quarter * 2 * np.pi), PI_32,
                                                 ALU.add, ALU.min))
                own.settle()
                nc.vector.tensor_scalar(r[:], r[:], -PI_32, None, ALU.max).then_inc(angle_ready, 1)
            wait_loads(dve, "others")
            nc.vector.tensor_copy(w["pairs"][:], pairs[:])
            low_parts(dve, nc.vector, range(first_dve, len(halves)))
            wait_loads(dve, "plain")
            nc.vector.tensor_scalar(w["b2h"][:], w["b2h"][:], 0.5, None, ALU.mult)

        @block.scalar
        def _(act):
            load(act, "moe")
            load(act, "down")
            wait_loads(act, "moe")
            for k, (whole, high, _) in enumerate(halves):
                if k == first_others:
                    wait_loads(act, "others")
                nc.scalar.activation(high, whole, ACT.Copy).then_inc(high_ready, 1)
            for n, f in enumerate(angle):
                act.wait_ge(angle_ready, n + 1)
                nc.scalar.activation(w[f + "_t"][:], angle[f][:], ACT.Sin).then_inc(table_ready, 1)
            for n, f in enumerate(angle):
                act.wait_ge(turned_ready, n + 1)
                nc.scalar.activation(w[f + "_c"][:], turned[f][:], ACT.Copy)

        @block.tensor
        def _(pe):
            wait_loads(pe, "tables")
            for n, f in enumerate(angle):
                pe.wait_ge(table_ready, n + 1)
                for t in range(T):
                    mm = pe.transpose(turned[f][:, t], w[f + "_t"][:, t], w["ident"][:])
                mm.then_inc(turned_ready, 1)
    return w


def lay_out(inputs):
    f = np.float32

    def rows(v, n=T):
        v = np.asarray(v).reshape(-1)
        return np.ascontiguousarray(np.broadcast_to(v, (P, n) + v.shape))

    def experts(v):
        return np.asarray(v).reshape(TE, 2, D, I_E).transpose(2, 0, 1, 3).reshape(D, TE, P)

    wq, wk = np.asarray(inputs["L1_attn_wq"]), np.asarray(inputs["L1_attn_wk"])
    q_rep, k_rep = np.zeros((D, GRP, HG, 4, DH), f), np.zeros((D, GRP, HG, 4, DH), f)
    for part in range(3):
        q_rep[:, :, :, part] = wq.reshape(D, GRP, HG, DH)
        k_rep[:, :, :, part] = wk.reshape(D, GRP, HG, DH)
    tok = np.arange(P)
    pos = (T * tok[:, None] + np.arange(T)[None, :]).astype(f)
    theta = np.asarray(inputs["L0_attn_theta"]).reshape(D)
    bias = np.asarray(inputs["L0_attn_bqkvu"])
    keep = np.zeros((P, 5), f)
    r = np.arange(P) % 32
    part = r // DH
    keep[:, 0] = np.where(part == 1, -1, 1)
    keep[:, 1] = part == 1
    keep[:, 2] = np.where(part == 2, -1, 1)
    keep[:, 3] = part == 2
    keep[:, 4] = r == MAX_ROW
    head = np.arange(P) // DH
    return {
        "x": np.asarray(inputs["L0_attn_x"]),
        "we_gate_t": experts(inputs["L0_ffn_We_gate"]), "we_up_t": experts(inputs["L0_ffn_We_up"]), "We_down": inputs["L0_ffn_We_down"],
        "Ws_gate": inputs["L0_ffn_Ws_gate"], "Ws_up": inputs["L0_ffn_Ws_up"], "Ws_down": inputs["L0_ffn_Ws_down"],
        "gate_t": np.asarray(inputs["L0_ffn_gate_weight"]).T,
        "wqkvu_t": np.asarray(inputs["L0_attn_Wqkvu"]).T,
        "wout_t": np.asarray(inputs["L0_attn_Wout"]).T,
        "bq": bias[:D, None], "bkvu": rows(bias[D:], 1)[:, 0], "bout": rows(inputs["L0_attn_bout"]),
        "lnw": rows(inputs["L0_attn_ln_w"]), "lnb": rows(inputs["L0_attn_ln_b"]),
        "w1": inputs["L1_ffn_w1"], "w2": inputs["L1_ffn_w2"],
        "b1": np.asarray(inputs["L1_ffn_b1"]).reshape(FT, P).T, "b2": rows(inputs["L1_ffn_b2"]),
        "lns": rows(inputs["L1_attn_ln_scale"]), "lnsb": rows(inputs["L1_attn_ln_bias"]),
        "wv": inputs["L1_attn_wv"],
        "q_rep": q_rep.reshape(D, GRP * P), "k_rep": k_rep.reshape(D, GRP * P),
        "theta_t": rows(theta), "c_pos_t": np.broadcast_to(pos[:, :, None], (P, T, P)),
        "c_ident": np.eye(P, dtype=f),
        "c_ramp": np.broadcast_to(np.arange(E, 0, -1, dtype=f), (P, T, E)),
        "c_heads": np.broadcast_to((head[:, None] == head[None, :]).astype(f)[:, None], (P, 2, D)),
        "c_pairs": (np.arange(2 * E)[:, None, None] % E == 2 * np.arange(TE)[None, :, None]
                    + (np.arange(P) // I_E)[None, None, :]).astype(f),
        "c_keep": keep,
    }


def kernel(**inputs):
    import concourse.bacc as bacc
    from concourse.bass_utils import run_bass_kernel_spmd

    nc = bacc.Bacc("TRN2", target_bir_lowering=False, num_devices=1)
    arrays, args = {}, {}
    for name, a in lay_out(inputs).items():
        a = np.ascontiguousarray(a)
        arrays[f"in_{name}"] = a
        args[name] = nc.dram_tensor(f"in_{name}", a.shape, mybir.dt.from_np(a.dtype), kind="ExternalInput").ap()
    shape = arrays["in_x"].shape
    assert shape == (NB, N, D)
    mid = nc.dram_tensor("mid", (PAD + NB, N, D), F32, kind="Internal").ap()
    out = nc.dram_tensor("out", shape, F32, kind="ExternalOutput").ap()
    with ExitStack() as back:
        with ExitStack() as front:
            w = build_weights(nc, front, back, args)
            build_front(nc, w, args["x"], mid, args["c_ident"], NB // 2)
        build_back(nc, w, mid, out, NB)
    r = run_bass_kernel_spmd(nc, [arrays], core_ids=[0])
    return r.results[0]["out"]
```
